# Optimizing a Trainium2 kernel written in Bass

```python
import numpy as np
import jax
import jax.numpy as jnp

def _softmax(x, axis=-1):
    return jax.nn.softmax(x, axis=axis)

def _gelu(x):
    return jax.nn.gelu(x, approximate=True)

def _silu(x):
    return jax.nn.silu(x)

def _sigmoid(x):
    return jax.nn.sigmoid(x)

def _layernorm(x, axis=-1, eps=1e-05):
    m = jnp.mean(x, axis=axis, keepdims=True)
    v = jnp.var(x, axis=axis, keepdims=True)
    return (x - m) / jnp.sqrt(v + eps)

def _scatter_add(tgt, idx, src, axis=0):
    return tgt.at[idx].add(src)

def _segment_sum(src, seg, n):
    return jax.ops.segment_sum(src, seg, n)
kernel_name = 'mk_xattn_ffn_d1_seqx_r4_49a15b'

def setup_inputs(seed: int=0):
    np.random.seed(seed)
    _w = jnp.asarray

    def _rec_inputs():
        import jax
        import jax.numpy as jnp
        _rk = jax.random.key(seed)
        x = -0.0003929 + 0.9999 * jax.random.normal(jax.random.fold_in(_rk, 1), (8, 256, 1024), jnp.float32)
        _lenS = 256 - jax.random.randint(jax.random.fold_in(_rk, 7), (8,), 0, max(1, 256 // 4) + 1, jnp.int32)
        _lenS2 = 256 - jax.random.randint(jax.random.fold_in(_rk, 8), (8,), 0, max(1, 256 // 4) + 1, jnp.int32)
        _ctx_4096P = jax.random.normal(jax.random.fold_in(_rk, 11), (8, 16, 1024), jnp.float32)
        _ctx_4096c = jax.random.dirichlet(jax.random.fold_in(_rk, 511), 0.3 * jnp.ones((16,), jnp.float32), (8, 256))
        _ctx_4096t = jnp.einsum('bsk,bkd->bsd', _ctx_4096c, _ctx_4096P)
        _ctx_4096t = _ctx_4096t * jax.lax.rsqrt(jnp.mean(jnp.square(_ctx_4096t)) + 1e-12) * 0.953939
        ctx_4096 = 2.81802e-05 + 1.00001 * (_ctx_4096t + 0.3 * jax.random.normal(jax.random.fold_in(_rk, 611), (8, 256, 1024), jnp.float32))
        _validS = jnp.arange(256)[None, :] < _lenS[:, None]
        _validS2 = jnp.arange(256)[None, :] < _lenS2[:, None]
        _causal = jnp.tril(jnp.ones((256, 256), dtype=bool))
        mask_BxSxS2_ff0 = jnp.where(jnp.ones((8, 256, 256), dtype=bool), 0.0, -1000000000.0).astype(jnp.float32)
        return (x, ctx_4096, mask_BxSxS2_ff0)
    x, ctx_4096, mask_BxSxS2_ff0 = _rec_inputs()

    def _L0_xattn_setup():
        import jax, jax.numpy as jnp
        import numpy as np
        B, S, D = (4, 256, 1024)
        HQ, HKV, DK, DV = (32, 8, 128, 128)

        def apply_rope(x, positions):
            d = x.shape[-1]
            inv_freq = 1.0 / 10000.0 ** (jnp.arange(0, d, 2, dtype=jnp.float32) / d)
            ang = positions.astype(jnp.float32)[:, None] * inv_freq[None, :]
            cos = jnp.cos(ang)[None, None]
            sin = jnp.sin(ang)[None, None]
            x1, x2 = (x[..., :d // 2], x[..., d // 2:])
            return jnp.concatenate([x1 * cos - x2 * sin, x2 * cos + x1 * sin], axis=-1)
        key = jax.random.key(seed)
        ks = jax.random.split(key, 8)
        return {'query': jax.random.normal(ks[0], (B, S, D), jnp.float32), 'key': jax.random.normal(ks[1], (B, S, D), jnp.float32), 'value': jax.random.normal(ks[2], (B, S, D), jnp.float32), 'mask': jnp.zeros((B, S, S), jnp.float32), 'wq': jax.random.normal(ks[3], (D, HQ * DK), jnp.float32) * 0.02, 'wk': jax.random.normal(ks[4], (D, HKV * DK), jnp.float32) * 0.02, 'wv': jax.random.normal(ks[5], (D, HKV * DV), jnp.float32) * 0.02, 'wo': jax.random.normal(ks[6], (HQ * DV, D), jnp.float32) * 0.02, 'curr_seq_pos': 0}
    _L0_xattn_all = _L0_xattn_setup()
    _L0_xattn_in = {k: v for k, v in _L0_xattn_all.items() if k in ('wq', 'wk', 'wv', 'wo')}
    del _L0_xattn_all

    def _L0_ffn_setup():
        import jax, jax.numpy as jnp
        import numpy as np
        B_L, B_H = (4, 8)
        LIN_SLOPE, LIN_INTER, EST_T = (1.0, 0.0, 64.0)
        BATCH, SEQ, IN_F, OUT_F = (4, 512, 1024, 1024)
        MAX_BITS = 8

        def dequant_kbit(qweight, lut, bit):
            O, I32 = (qweight.shape[1], qweight.shape[2])
            shifts = jnp.arange(32, dtype=jnp.int32)
            idx = jnp.zeros((O, I32 * 32), dtype=jnp.int32)
            for p in range(bit):
                bits = (qweight[p][:, :, None] >> shifts & 1).reshape(O, I32 * 32)
                idx = idx | bits << p
            return jnp.take_along_axis(lut, idx, axis=1)
        key = jax.random.key(seed)
        k = jax.random.split(key, 5)
        x = jax.random.normal(k[0], (BATCH, SEQ, IN_F), dtype=jnp.float32)
        qweight = jax.random.randint(k[1], (MAX_BITS, OUT_F, IN_F // 32), 0, 2147483647, dtype=jnp.int32)
        lut4 = jax.random.normal(k[2], (OUT_F, 2 ** B_L), dtype=jnp.float32) * 0.02
        lut8 = jax.random.normal(k[3], (OUT_F, 2 ** B_H), dtype=jnp.float32) * 0.02
        bias = jax.random.normal(k[4], (OUT_F,), dtype=jnp.float32) * 0.01
        return {'x': x, 'qweight': qweight, 'lut4': lut4, 'lut8': lut8, 'bias': bias}
    _L0_ffn_all = _L0_ffn_setup()
    _L0_ffn_in = {k: v for k, v in _L0_ffn_all.items() if k in ('qweight', 'lut4', 'lut8', 'bias')}
    del _L0_ffn_all
    return {'x': x, 'ctx_4096': ctx_4096, 'mask_BxSxS2_ff0': mask_BxSxS2_ff0, 'L0_xattn_wq': _L0_xattn_in['wq'], 'L0_xattn_wk': _L0_xattn_in['wk'], 'L0_xattn_wv': _L0_xattn_in['wv'], 'L0_xattn_wo': _L0_xattn_in['wo'], 'L0_ffn_qweight': _L0_ffn_in['qweight'], 'L0_ffn_lut4': _L0_ffn_in['lut4'], 'L0_ffn_lut8': _L0_ffn_in['lut8'], 'L0_ffn_bias': _L0_ffn_in['bias']}

def reference(x, ctx_4096, mask_BxSxS2_ff0, L0_xattn_wq, L0_xattn_wk, L0_xattn_wv, L0_xattn_wo, L0_ffn_qweight, L0_ffn_lut4, L0_ffn_lut8, L0_ffn_bias):
    import jax
    import jax.numpy as jnp

    def _L0_xattn_ref(query, key, value, mask, wq, wk, wv, wo, curr_seq_pos):
        import jax, jax.numpy as jnp
        import numpy as np
        B, S, D = (4, 256, 1024)
        HQ, HKV, DK, DV = (32, 8, 128, 128)

        def apply_rope(x, positions):
            d = x.shape[-1]
            inv_freq = 1.0 / 10000.0 ** (jnp.arange(0, d, 2, dtype=jnp.float32) / d)
            ang = positions.astype(jnp.float32)[:, None] * inv_freq[None, :]
            cos = jnp.cos(ang)[None, None]
            sin = jnp.sin(ang)[None, None]
            x1, x2 = (x[..., :d // 2], x[..., d // 2:])
            return jnp.concatenate([x1 * cos - x2 * sin, x2 * cos + x1 * sin], axis=-1)
        bs, sq, _ = query.shape
        sk = key.shape[1]
        n_groups = HQ // HKV
        q = (query @ wq).reshape(bs, sq, HQ, DK).transpose(0, 2, 1, 3)
        k = (key @ wk).reshape(bs, sk, HKV, DK)
        v = (value @ wv).reshape(bs, sk, HKV, DV)
        k = jnp.repeat(k, n_groups, axis=2).transpose(0, 2, 1, 3)
        v = jnp.repeat(v, n_groups, axis=2).transpose(0, 2, 1, 3)
        scale = jnp.sqrt(jnp.float32(DK))
        pos = curr_seq_pos + jnp.arange(sq)
        q = apply_rope(q, pos)
        k = apply_rope(k, curr_seq_pos + jnp.arange(sk))
        scores = jnp.einsum('bhqd,bhkd->bhqk', q, k) / scale
        m = jax.lax.dynamic_slice(mask, (0, curr_seq_pos, 0), (bs, sq, sk))
        attn = jax.nn.softmax(scores + m[:, None, :, :], axis=-1)
        out = jnp.einsum('bhqk,bhkd->bhqd', attn, v)
        out = out.transpose(0, 2, 1, 3).reshape(bs, sq, HQ * DV)
        return out @ wo

    def _L0_ffn_ref(x, qweight, lut4, lut8, bias):
        import jax, jax.numpy as jnp
        import numpy as np
        B_L, B_H = (4, 8)
        LIN_SLOPE, LIN_INTER, EST_T = (1.0, 0.0, 64.0)
        BATCH, SEQ, IN_F, OUT_F = (4, 512, 1024, 1024)
        MAX_BITS = 8

        def dequant_kbit(qweight, lut, bit):
            O, I32 = (qweight.shape[1], qweight.shape[2])
            shifts = jnp.arange(32, dtype=jnp.int32)
            idx = jnp.zeros((O, I32 * 32), dtype=jnp.int32)
            for p in range(bit):
                bits = (qweight[p][:, :, None] >> shifts & 1).reshape(O, I32 * 32)
                idx = idx | bits << p
            return jnp.take_along_axis(lut, idx, axis=1)
        e = jnp.linalg.norm(x, axis=-1) * LIN_SLOPE + LIN_INTER
        mask = e > EST_T
        w_l = dequant_kbit(qweight, lut4, B_L)
        w_h = dequant_kbit(qweight, lut8, B_H)
        y_l = jnp.einsum('bsi,oi->bso', x, w_l)
        y_h = jnp.einsum('bsi,oi->bso', x, w_h)
        y = jnp.where(mask[..., None], y_h, y_l) + bias
        return y
    x = x + _L0_xattn_ref(_layernorm(x, axis=-1), ctx_4096, ctx_4096, mask_BxSxS2_ff0, L0_xattn_wq, L0_xattn_wk, L0_xattn_wv, L0_xattn_wo, 0)
    x = x + _L0_ffn_ref(_layernorm(x, axis=-1), L0_ffn_qweight, L0_ffn_lut4, L0_ffn_lut8, L0_ffn_bias)
    return x

_drawn_inputs = setup_inputs


def setup_inputs(seed=0):
    import zlib

    import numpy as np

    out = dict(_drawn_inputs(seed))
    spreads = {}
    factors = {'L0_ffn_bias': 7.201}
    for name, (base, spread) in spreads.items():
        noise = np.random.default_rng([zlib.crc32(name.encode()), seed]).standard_normal(out[name].shape)
        drawn = base * np.exp(spread * noise) if base else spread * noise
        out[name] = jnp.asarray(drawn.astype(out[name].dtype))
    for name, factor in factors.items():
        out[name] = (out[name] * factor).astype(out[name].dtype)
    return out
```

```python
class Steps:

    def __init__(self, eng, sem, base):
        self.eng, self.sem, self.base, self.n = eng, sem, base, 0

    def mark(self, instruction):
        instruction.then_inc(self.sem, 1)
        self.n += 1

    def wait(self):
        self.eng.wait_ge(self.sem, self.base + self.n)


def build_xattn_ffn(nc, x, ctx, mask, wq, wk, wv, wo, qweight, lut4, bias, rope_cos, rope_sin, out):
    from contextlib import ExitStack

    from concourse import mybir

    F32, F32R, I32 = mybir.dt.float32, mybir.dt.float32r, mybir.dt.int32
    ALU, ACT = mybir.AluOpType, mybir.ActivationFunctionType

    P = 128
    NB, S, D = x.shape
    DK = P
    HQ, HKV = wq.shape[1] // DK, wk.shape[1] // DK
    REP = HQ // HKV
    C = D // P
    TS = S // P
    NH = 2
    HB = NB // NH
    HT = HB * TS
    UNITS = HB * REP
    BITS = 4
    LEVELS = 1 << BITS
    WORDS = D // 32
    BANK = 512
    NN = D // BANK
    EPS = 1e-5
    SCALE = float(DK) ** -0.5
    HI, LO = 0, 1
    PASSES = ((HI, HI), (HI, LO), (LO, HI))
    assert (S, DK, TS, NN, REP, HB, C) == (256, 128, 2, 2, 4, 4, 8)

    A_ROPES = NB * HKV
    HALF_UNITS = HKV * UNITS
    A_WIDE = NB * TS * NN
    BURST = TS * NN
    HALF_WIDE = HKV * HB * BURST + HT * NN
    A_PIECES = 2 * C
    HALF_PIECES = REP + HKV * 2 * REP
    V_USES = TS * NN + 2
    DQ_STEPS = 1 + (BITS - 1) + 1 + 2 * (LEVELS // 2 - 1)
    LN_STEPS = 2 + 4

    x_tiles = x.rearrange("b (t p) d -> (b t) p d", p=P)
    out_tiles = out.rearrange("b (t p) d -> (b t) p d", p=P)
    ctx_tiles = ctx.rearrange("b (t p) d -> b t p d", p=P)
    mask_v = mask.rearrange("b (t p) k -> b p t k", p=P)
    wk_v = wk.rearrange("(c p) n -> c p n", p=P)
    wv_v = wv.rearrange("(c p) n -> c p n", p=P)
    wq_v = wq.rearrange("(c p) (h n) -> h p c n", p=P, n=DK)
    wo_v = wo.rearrange("(h p) n -> h p n", p=DK)
    qw_v = qweight[0:BITS].rearrange("k (t p) w -> t p k w", p=P)
    lut_v = lut4.rearrange("(t p) l -> t p l", p=P)
    bias_v = bias.rearrange("(a n) -> a n", a=1)
    k_scr = nc.dram_tensor("k_scratch", (HKV, NB, P, 2 * S), F32, kind="Internal").ap()
    v_scr = nc.dram_tensor("v_scratch", (NB, TS, 2, P, HKV * DK), F32, kind="Internal").ap()
    w_scr = nc.dram_tensor("w_scratch", (P, C, 2, D), F32, kind="Internal").ap()

    with ExitStack() as stack:
        def sb(name, shape, dt):
            return stack.enter_context(nc.sbuf_tensor(name, shape, dt))

        def sem(name):
            return stack.enter_context(nc.semaphore(name))

        W = sb("weights_split", [P, 2 * C * D], F32R)
        X = sb("acts_split", [P, 2 * C * D], F32R)
        R = sb("small_split", [P, 6144], F32R)
        wk_s = W[:, :].rearrange("p (c l n) -> p c l n", c=C, l=2)
        wv_s = X[:, :].rearrange("p (c l n) -> p c l n", c=C, l=2)
        ctxT = R[:, 0:4096].rearrange("p (c l n) -> p c l n", c=C, l=2)
        k_stage = R[:, 4096:5120].rearrange("p (s l n) -> p s l n", s=2, l=2)
        v_stage = R[:, 5120:6144].rearrange("p (l n) -> p l n", l=2)
        wq_s = W[:, 0:8192].rearrange("p (h c l n) -> p h c l n", h=REP, c=C, l=2)
        wo_s = W[:, 8192:16384].rearrange("p (h l n) -> p h l n", h=REP, l=2)
        xT = X[:, :].rearrange("p (c l n) -> p c l n", c=C, l=2)
        q_s = R[:, 0:2048].rearrange("p (s l n) -> p s l n", s=4, l=2)
        o_s = R[:, 2048:4096].rearrange("p (h l n) -> p h l n", h=REP, l=2)
        k_s = R[:, 4096:4608].rearrange("p (l n) -> p l n", l=2)
        v_s = R[:, 4608:5120].rearrange("p (k l n) -> p k l n", k=TS, l=2)
        pT_s = R[:, 5120:6144].rearrange("p (l k n) -> p l k n", l=2, k=TS)
        w4_s = W[:, :].rearrange("p (c l n) -> p c l n", c=C, l=2)

        acc_t = sb("residual", [P, HT * D], F32)
        acc = acc_t[:, :].rearrange("p (t n) -> p t n", t=HT)
        ctx_stage = acc_t[:, 0:2048].rearrange("p (t n) -> p t n", t=TS)
        codes = acc_t[:, 2048:3072].bitcast(I32)
        term_v = acc_t[:, 3072:4096]
        sum_v = acc_t[:, 4096:5120]
        term_p = acc_t[:, 5120:6144]
        sum_p = acc_t[:, 6144:7168]
        planes = acc_t[:, 7168:7296].bitcast(I32).rearrange("p (k w) -> p k w", k=BITS)
        spread = acc_t[:, 7296:7808].bitcast(I32).rearrange("p (r k w) -> p r k w", r=4, k=BITS)
        nibbles = acc_t[:, 7808:7936].bitcast(I32).rearrange("p (r w) -> p r w", r=4)
        lut_t = acc_t[:, 7936:7936 + LEVELS]
        raw_t = sb("raw", [P, 2 * D], F32)
        raw = raw_t[:, :].rearrange("p (s n) -> p s n", s=2)
        prob_t = sb("probs", [P, 2 * TS * S], F32)
        probs = prob_t[:, :].rearrange("p (s t k) -> p s t k", s=2, t=TS)
        bias_t = prob_t[:, :]
        mask_t = sb("mask_tile", [P, TS, S], F32)
        rope_x = sb("rope_x", [P, S], F32)
        rope_a = sb("rope_a", [P, S], F32)
        rope_b = sb("rope_b", [P, S], F32)
        cos_t = sb("cos_t", [P, S], F32)
        sin_t = sb("sin_t", [P, S], F32)
        ident = sb("ident", [P, P], F32)
        neg_max = sb("neg_max", [P, 2, TS], F32)
        row_max = sb("row_max", [P, 2, TS], F32)
        row_sum = sb("row_sum", [P, 2, TS], F32)
        row_inv = sb("row_inv", [P, 2, TS], F32)
        ln_stat = sb("ln_stat", [P, 2, 2, 6], F32)
        ln_mv = sb("ln_mv", [P, 2, 2], F32)
        ln_ve = sb("ln_ve", [P, 2], F32)
        ln_sd = sb("ln_sd", [P, 2], F32)
        ln_y = sb("ln_y", [P, 2], F32)
        ln_e = sb("ln_e", [P, 2], F32)
        ln_f = sb("ln_f", [P, 2], F32)
        ln_r = sb("ln_r", [P, 2], F32)

        bank = [stack.enter_context(nc.psum_tensor(f"bank{i}", [P, BANK], F32)) for i in range(8)]
        ctx_ps = [bank[i] for i in (0, 1, 2, 5)]
        w4_ps = [bank[0], bank[1]]
        rope_ps = [bank[3], bank[4]]
        wide_ps = [bank[6], bank[7]]
        s_ps = [bank[0], bank[1]]
        pT_ps = bank[2]
        o_ps = bank[5]
        ln_ps = [(bank[0], bank[1]), (bank[2], bank[5])]

        tables_in = sem("tables_in")
        ctx_in = [sem(f"ctx_in{t}") for t in range(TS)]
        quant_in = sem("quant_in")
        raw_in = [sem(f"raw_in{s}") for s in range(2)]
        x_in = [sem(f"x_in{t}") for t in range(HT)]
        k_in, v_in, mask_in = sem("k_in"), sem("v_in"), sem("mask_in")
        w4_in = [sem(f"w4_in{j}") for j in range(4)]
        bias_in = sem("bias_in")
        k_stored = [sem(f"k_stored{s}") for s in range(2)]
        v_stored = sem("v_stored")
        out_stored = sem("out_stored")
        ident_step, ident_ok = sem("ident_step"), sem("ident_ok")
        w_hi, w_lo = sem("w_hi"), sem("w_lo")
        ctx_tr, ctx_hi, ctx_lo = sem("ctx_tr"), sem("ctx_hi"), sem("ctx_lo")
        stage_hi, stage_lo = sem("stage_hi"), sem("stage_lo")
        dq_step = sem("dq_step")
        term_ready, term_used = sem("term_ready"), sem("term_used")
        w4_ready, w4_tr = sem("w4_ready"), sem("w4_tr")
        rope_mm, rope_in = sem("rope_mm"), sem("rope_in")
        rope_cosd, rope_sind = sem("rope_cosd"), sem("rope_sind")
        rope_sum, rope_hi, rope_lo = sem("rope_sum"), sem("rope_hi"), sem("rope_lo")
        wide_mm, wide_free = sem("wide_mm"), sem("wide_free")
        s_mm, s_read, s_max = sem("s_mm"), sem("s_read"), sem("s_max")
        exp_done, inv_ready, inv_max = sem("exp_done"), sem("inv_ready"), sem("inv_max")
        p_ready, pT_tr, pT_hi, pT_lo = sem("p_ready"), sem("pT_tr"), sem("pT_hi"), sem("pT_lo")
        o_mm, o_hi, o_lo = sem("o_mm"), sem("o_hi"), sem("o_lo")
        ln_step, ln_var, ln_std = sem("ln_step"), sem("ln_var"), sem("ln_std")
        ln_rows, ln_tr, ln_hi, ln_lo = sem("ln_rows"), sem("ln_tr"), sem("ln_hi"), sem("ln_lo")
        biased, out_ready = sem("biased"), sem("out_ready")
        held = sem("held")

        def hold(eng):
            eng.sem_inc(held, 1)

        block = stack.enter_context(nc.Block())

        @block.sync
        def _(sp):
            def load_raw(k, src, slot, first=False):
                if not first:
                    sp.wait_ge(w_lo, k - 1)
                dst = raw[:, slot, :]
                if len(src.shape) == 3:
                    dst = dst.rearrange("p (c n) -> p c n", c=C)
                sp.dma_start(dst, src).then_inc(raw_in[slot], 16)

            def load_quant(t):
                sp.dma_start(planes, qw_v[t]).then_inc(quant_in, 16)
                sp.dma_start(lut_t, lut_v[t]).then_inc(quant_in, 16)

            for t in range(TS):
                sp.dma_start(ctx_stage[:, t, :], ctx_tiles[0, t]).then_inc(ctx_in[t], 16)
            for c in range(C):
                load_raw(c, wk_v[c], c % 2, first=c < 2)
            sp.dma_start(cos_t[:, :], rope_cos).then_inc(tables_in, 16)
            sp.dma_start(sin_t[:, :], rope_sin).then_inc(tables_in, 16)
            load_quant(0)
            for c in range(C):
                load_raw(C + c, wv_v[c], c % 2)
            with sp.Fori(0, NB) as b:
                following = sp.snap((b + 1) % NB)
                for g in range(HKV):
                    sp.wait_ge(rope_lo, 1 + b * HKV + g + 1)
                    sp.dma_start(k_scr[g, b], k_stage[:, g % 2].bitcast(F32)
                                 .rearrange("p l n -> p (l n)")).then_inc(k_stored[g % 2], 16)
                sp.wait_ge(ctx_tr, 4 * b + 4)
                for t in range(TS):
                    sp.dma_start(ctx_stage[:, t, :], ctx_tiles[following, t]).then_inc(ctx_in[t], 16)
                for t in range(TS):
                    for n in range(NN):
                        sp.wait_ge(stage_lo, b * V_USES + t * NN + n + 1)
                        sp.dma_start(v_scr[b, t, :, :, n * BANK:(n + 1) * BANK].rearrange("l p n -> p l n"),
                                     v_stage.bitcast(F32)).then_inc(v_stored, 16)
                for j in range(2):
                    sp.wait_ge(stage_lo, b * V_USES + TS * NN + j + 1)
                    dst = w_scr.rearrange("p c l (t n) -> t l p c n", n=P)
                    for l in (HI, LO):
                        sp.dma_start(dst[b, l, :, 4 * j:4 * j + 4, :],
                                     v_stage[:, l, :].bitcast(F32).rearrange("p (c n) -> p c n", c=4)
                                     ).then_inc(v_stored, 16)
                load_quant(following)
            for s in range(2):
                sp.wait_ge(k_stored[s], 16 + 16 * NB * HKV // 2)
            sp.wait_ge(v_stored, 32 + 16 * NB * (V_USES + 2))
            for t in range(TS):
                sp.wait_ge(ctx_in[t], 16 * (NB + 1))
            sp.wait_ge(quant_in, 32 * (NB + 1))

            with sp.Fori(0, NH) as hf:
                piece = A_PIECES + hf * HALF_PIECES
                for t in range(HT):
                    sp.dma_start(acc[:, t, :], x_tiles[hf * HT + t]).then_inc(x_in[t], 16)
                for h in range(REP):
                    load_raw(piece + h, wq_v[h], h % 2)
                with sp.Fori(0, HKV) as g:
                    after = sp.snap((g + 1) % HKV)
                    n0 = hf * HALF_UNITS + g * UNITS
                    for b in range(HB):
                        batch = hf * HB + b
                        n = n0 + b * REP
                        sp.wait_ge(s_mm, n + 1)
                        hold(sp)
                        sp.dma_start(k_s.bitcast(F32).rearrange("p l n -> p (l n)"),
                                     k_scr[g, batch]).then_inc(k_in, 16)
                        sp.wait_ge(s_read, n + 2)
                        hold(sp)
                        sp.dma_start(mask_t[:, :, :], mask_v[batch]).then_inc(mask_in, 16)
                        sp.wait_ge(o_mm, n + 1)
                        hold(sp)
                        v_src = v_scr[batch].rearrange("k l p (g n) -> g p (k l) n", n=DK)
                        sp.dma_start(v_s.bitcast(F32).rearrange("p k l n -> p (k l) n"),
                                     v_src[g]).then_inc(v_in, 16)
                        if b == 0:
                            sp.wait_ge(ln_tr, 2 + hf * 2 * HT + HT)
                            hold(sp)
                            for h in range(REP):
                                load_raw(piece + REP + g * 2 * REP + h, wo_v[g * REP + h], h % 2)
                        if b >= 2:
                            for h in (2 * b - 4, 2 * b - 3):
                                load_raw(piece + 2 * REP + g * 2 * REP + h, wq_v[after * REP + h], h % 2)
                sp.wait_ge(wide_mm, A_WIDE + hf * HALF_WIDE + HKV * HB * BURST)
                hold(sp)
                sp.wait_ge(w_lo, piece + HALF_PIECES)
                hold(sp)
                for j in range(4):
                    sp.dma_start(w4_s[:, 2 * j:2 * j + 2].bitcast(F32).rearrange("p c l n -> p (c l n)"),
                                 w_scr[:, 2 * j:2 * j + 2].rearrange("p c l n -> p (c l n)")
                                 ).then_inc(w4_in[j], 16)
                sp.wait_ge(pT_tr, 2 + (hf + 1) * HALF_UNITS)
                sp.dma_start(bias_t, bias_v.to_broadcast([P, D])).then_inc(bias_in, 16)
                for t in range(HT):
                    sp.wait_ge(out_ready, hf * HT + t + 1)
                    sp.dma_start(out_tiles[hf * HT + t], acc[:, t, :]).then_inc(out_stored, 16)
                sp.wait_ge(out_stored, 16 * HT * (hf + 1))
                hold(sp)

        @block.tensor
        def _(pe):
            pe.sem_inc(s_mm, 1)
            pe.sem_inc(o_mm, 1)
            pe.sem_inc(pT_tr, 2)
            pe.sem_inc(ln_tr, 2)
            pe.wait_ge(ident_ok, 1)

            with pe.Fori(0, NB) as b:
                for t in range(TS):
                    pe.wait_ge(ctx_in[t], 16 * (b + 1))
                    for c in range(C):
                        col = (c % 2) * S + t * P
                        last = pe.transpose(ctx_ps[c // 2][:, col:col + P],
                                            ctx_stage[:, t, c * P:(c + 1) * P], ident[:, :])
                        if t == TS - 1 and c % 2:
                            last.then_inc(ctx_tr, 1)
                for g in range(HKV):
                    pe.wait_ge(rope_in, b * HKV + g + 1)
                    for c in range(C):
                        if g == 0:
                            pe.wait_ge(w_lo, c + 1)
                            pe.wait_ge(ctx_lo, 4 * b + c // 2 + 1)
                        for i, (a, m) in enumerate(PASSES):
                            last = pe.matmul(rope_ps[g % 2][:, 0:S], wk_s[:, c, a, g * DK:(g + 1) * DK],
                                             ctxT[:, c, m, :], start=c == 0 and i == 0,
                                             stop=c == C - 1 and i == 2)
                    last.then_inc(rope_mm, 1)
                pe.wait_ge(w_lo, A_PIECES)
                for t in range(TS):
                    for n in range(NN):
                        if t >= 1:
                            pe.wait_ge(stage_lo, b * V_USES + (t - 1) * NN + n + 1)
                        for c in range(C):
                            for i, (a, m) in enumerate(PASSES):
                                last = pe.matmul(wide_ps[n][:, :], ctxT[:, c, a, t * P:(t + 1) * P],
                                                 wv_s[:, c, m, n * BANK:(n + 1) * BANK],
                                                 start=c == 0 and i == 0, stop=c == C - 1 and i == 2)
                        last.then_inc(wide_mm, 1)
                pe.wait_ge(w4_ready, b + 1)
                for c in range(C):
                    last = pe.transpose(w4_ps[c // 4][:, (c % 4) * P:(c % 4 + 1) * P],
                                        sum_v[:, c * P:(c + 1) * P], ident[:, :])
                    if c % 4 == 3:
                        last.then_inc(w4_tr, 1)
                pe.wait_ge(stage_lo, (b + 1) * V_USES)

            def layernorm_tile(at, t):
                pe.wait_ge(ln_rows, at + t + 1)
                pe.wait_ge(ln_lo, at + t + 1)
                for c in range(C):
                    last = pe.transpose(ln_ps[t % 2][c // 4][:, (c % 4) * P:(c % 4 + 1) * P],
                                        raw[:, t % 2, c * P:(c + 1) * P], ident[:, :])
                last.then_inc(ln_tr, 1)

            with pe.Fori(0, NH) as hf:
                piece = A_PIECES + hf * HALF_PIECES
                wide0 = A_WIDE + hf * HALF_WIDE
                for t in range(HT):
                    layernorm_tile(hf * 2 * HT, t)
                pe.wait_ge(ln_lo, 2 + hf * 2 * HT + HT)
                hold(pe)

                with pe.Fori(0, HKV) as g:
                    n0 = hf * HALF_UNITS + g * UNITS
                    w0 = wide0 + g * HB * BURST

                    def query(u):
                        b, h = u // REP, u % REP
                        if b == 0:
                            pe.wait_ge(w_lo, piece + g * 2 * REP + h + 1)
                        pe.wait_ge(rope_in, A_ROPES + n0 + u + 1)
                        for c in range(C):
                            for i, (a, m) in enumerate(PASSES):
                                last = pe.matmul(rope_ps[u % 2][:, 0:S], wq_s[:, h, c, a, :],
                                                 xT[:, c, m, b * S:(b + 1) * S],
                                                 start=c == 0 and i == 0, stop=c == C - 1 and i == 2)
                        last.then_inc(rope_mm, 1)

                    def scores(u):
                        if u % REP == 0:
                            pe.wait_ge(k_in, 16 * (hf * HKV * HB + g * HB + u // REP + 1))
                        pe.wait_ge(rope_lo, 1 + A_ROPES + n0 + u + 1)
                        pe.wait_ge(s_read, n0 + u + 1)
                        for t in range(TS):
                            for i, (a, m) in enumerate(PASSES):
                                last = pe.matmul(s_ps[u % 2][:, t * S:(t + 1) * S],
                                                 q_s[:, u % 4, a, t * P:(t + 1) * P], k_s[:, m, :],
                                                 start=i == 0, stop=i == 2)
                        last.then_inc(s_mm, 1)

                    def turn(u):
                        pe.wait_ge(p_ready, n0 + u + 1)
                        pe.wait_ge(pT_lo, n0 + u + 1)
                        for t in range(TS):
                            for k in range(TS):
                                last = pe.transpose(pT_ps[:, k * S + t * P:k * S + (t + 1) * P],
                                                    probs[:, u % 2, t, k * P:(k + 1) * P], ident[:, :])
                        last.then_inc(pT_tr, 1)

                    def attend(u):
                        if u % REP == 0:
                            pe.wait_ge(v_in, 16 * (hf * HKV * HB + g * HB + u // REP + 1))
                        pe.wait_ge(pT_lo, 1 + n0 + u + 1)
                        pe.wait_ge(o_lo, n0 + u + 1)
                        for k in range(TS):
                            for i, (a, m) in enumerate(PASSES):
                                last = pe.matmul(o_ps[:, 0:S], v_s[:, k, a, :], pT_s[:, m, k, :],
                                                 start=k == 0 and i == 0, stop=k == TS - 1 and i == 2)
                        last.then_inc(o_mm, 1)

                    def project(b):
                        if b == 0:
                            pe.wait_ge(w_lo, piece + REP + g * 2 * REP + REP)
                        pe.wait_ge(o_lo, 1 + n0 + (b + 1) * REP)
                        for t in range(TS):
                            for n in range(NN):
                                pe.wait_ge(wide_free, w0 - A_WIDE + b * BURST + t * NN + n + 1)
                                for h in range(REP):
                                    for i, (a, m) in enumerate(PASSES):
                                        last = pe.matmul(wide_ps[n][:, :], o_s[:, h, a, t * P:(t + 1) * P],
                                                         wo_s[:, h, m, n * BANK:(n + 1) * BANK],
                                                         start=h == 0 and i == 0,
                                                         stop=h == REP - 1 and i == 2)
                                last.then_inc(wide_mm, 1)

                    query(0)
                    query(1)
                    for u in range(UNITS):
                        scores(u)
                        if u >= 6 and u % REP == 2:
                            project(u // REP - 1)
                        if u + 2 < UNITS:
                            query(u + 2)
                        if u >= 2:
                            attend(u - 2)
                        if u >= 1:
                            turn(u - 1)
                    attend(UNITS - 2)
                    turn(UNITS - 1)
                    attend(UNITS - 1)
                    project(HB - 1)

                at = hf * 2 * HT + HT
                layernorm_tile(at, 0)
                for t in range(HT):
                    if t + 1 < HT:
                        layernorm_tile(at, t + 1)
                    pe.wait_ge(ln_lo, 2 + at + t + 1)
                    for n in range(NN):
                        pe.wait_ge(wide_free, wide0 - A_WIDE + HKV * HB * BURST + t * NN + n + 1)
                        for c in range(C):
                            if t == 0 and n == 0 and c % 2 == 0:
                                pe.wait_ge(w4_in[c // 2], 16 * (hf + 1))
                            for i, (a, m) in enumerate(PASSES):
                                last = pe.matmul(wide_ps[n][:, :], xT[:, c, a, t * P:(t + 1) * P],
                                                 w4_s[:, c, m, n * BANK:(n + 1) * BANK],
                                                 start=c == 0 and i == 0, stop=c == C - 1 and i == 2)
                        last.then_inc(wide_mm, 1)

        @block.scalar
        def _(act):
            act.sem_inc(rope_in, 2)

            def split_hi(k, slot, dst, pieces=None):
                act.wait_ge(raw_in[slot], 16 * (k // 2 + 1) if isinstance(k, int) else pieces)
                src = raw[:, slot, :]
                if len(dst.shape) == 3:
                    src = src.rearrange("p (c n) -> p c n", c=C)
                act.activation(dst, src, ACT.Copy).then_inc(w_hi, 1)

            def rope_copy(n, slot, scale):
                act.wait_ge(rope_cosd, n + 1)
                act.wait_ge(rope_sind, n + 1)
                act.wait_ge(rope_mm, n + 1)
                act.activation(rope_x[:, :], rope_ps[slot][:, 0:S], ACT.Copy, scale=scale).then_inc(rope_in, 1)

            def rope_high(n, dst):
                act.wait_ge(rope_sum, n + 1)
                act.activation(dst, rope_a[:, :], ACT.Copy).then_inc(rope_hi, 1)

            for c in range(C):
                split_hi(c, c % 2, wk_s[:, c, HI, :])
            for c in range(C):
                split_hi(C + c, c % 2, wv_s[:, c, HI, :])
            with act.Fori(0, NB) as b:
                for j in range(4):
                    act.wait_ge(ctx_tr, 4 * b + j + 1)
                    act.activation(ctxT[:, 2 * j:2 * j + 2, HI, :],
                                   ctx_ps[j][:, :].rearrange("p (c n) -> p c n", c=2),
                                   ACT.Copy).then_inc(ctx_hi, 1)
                rope_copy(b * HKV, 0, 1.0)
                for g in range(HKV):
                    if g + 1 < HKV:
                        rope_copy(b * HKV + g + 1, (g + 1) % 2, 1.0)
                    act.wait_ge(k_stored[g % 2], 16 * (b * (HKV // 2) + g // 2 + 1))
                    rope_high(b * HKV + g, k_stage[:, g % 2, HI, :])
                for t in range(TS):
                    for n in range(NN):
                        act.wait_ge(v_stored, 16 * (b * (V_USES + 2) + t * NN + n) + 32)
                        act.wait_ge(wide_mm, (b * TS + t) * NN + n + 1)
                        act.activation(v_stage[:, HI, :], wide_ps[n][:, :], ACT.Copy).then_inc(stage_hi, 1)
                for j in range(2):
                    act.wait_ge(v_stored, 16 * (b * (V_USES + 2) + TS * NN + 2 * j) + 32)
                    act.wait_ge(w4_tr, b * 2 + j + 1)
                    act.activation(v_stage[:, HI, :], w4_ps[j][:, :], ACT.Copy).then_inc(stage_hi, 1)

            def layernorm_std(at, t):
                act.wait_ge(ln_var, at + t + 1)
                act.activation(ln_sd[:, t % 2:t % 2 + 1], ln_ve[:, t % 2:t % 2 + 1], ACT.Sqrt).then_inc(ln_std, 1)

            def layernorm_high(at, t):
                act.wait_ge(ln_tr, 2 + at + t + 1)
                for j in range(2):
                    last = act.activation(xT[:, 4 * j:4 * j + 4, HI, t * P:(t + 1) * P],
                                          ln_ps[t % 2][j][:, :].rearrange("p (c n) -> p c n", c=4), ACT.Copy)
                last.then_inc(ln_hi, 1)

            def layernorm(at):
                layernorm_std(at, 0)
                for t in range(HT):
                    if t + 1 < HT:
                        layernorm_std(at, t + 1)
                    layernorm_high(at, t)

            with act.Fori(0, NH) as hf:
                piece2 = A_PIECES // 2 + hf * (HALF_PIECES // 2)
                wide0 = A_WIDE + hf * HALF_WIDE
                act.wait_ge(wide_mm, wide0)
                for h in range(REP):
                    split_hi(None, h % 2, wq_s[:, h, :, HI, :], 16 * (piece2 + h // 2 + 1))
                layernorm(hf * 2 * HT)

                with act.Fori(0, HKV) as g:
                    n0 = hf * HALF_UNITS + g * UNITS
                    p0 = piece2 + REP // 2 + g * REP

                    def exponent(u):
                        act.wait_ge(s_max, n0 + u + 1)
                        for t in range(TS):
                            last = act.activation(probs[:, u % 2, t, :], probs[:, u % 2, t, :], ACT.Exp,
                                                  bias=neg_max[:, u % 2, t:t + 1],
                                                  accum_out=row_sum[:, u % 2, t:t + 1])
                        last.then_inc(exp_done, 1)

                    def turned_high(u):
                        act.wait_ge(o_mm, n0 + u + 1)
                        act.wait_ge(pT_tr, 2 + n0 + u + 1)
                        act.activation(pT_s[:, HI, :, :], pT_ps[:, :].rearrange("p (k n) -> p k n", k=TS),
                                       ACT.Copy).then_inc(pT_hi, 1)

                    def output_high(u):
                        b, h = u // REP, u % REP
                        if h == 0:
                            act.wait_ge(wide_mm, wide0 + (g * HB + b) * BURST)
                        act.wait_ge(o_mm, 1 + n0 + u + 1)
                        act.activation(o_s[:, h, HI, :], o_ps[:, 0:S], ACT.Copy).then_inc(o_hi, 1)

                    def query_high(u):
                        rope_high(A_ROPES + n0 + u, q_s[:, u % 4, HI, :])

                    rope_copy(A_ROPES + n0, 0, SCALE)
                    rope_copy(A_ROPES + n0 + 1, 1, SCALE)
                    query_high(0)
                    query_high(1)
                    for u in range(UNITS):
                        exponent(u)
                        if u < REP:
                            if u == 0:
                                act.wait_ge(wide_mm, wide0 + g * HB * BURST)
                            split_hi(None, u % 2, wo_s[:, u, HI, :], 16 * (p0 + u // 2 + 1))
                        if u >= UNITS - REP:
                            h = u - (UNITS - REP)
                            act.wait_ge(rope_mm, A_ROPES + n0 + u + 1)
                            split_hi(None, h % 2, wq_s[:, h, :, HI, :], 16 * (p0 + REP // 2 + h // 2 + 1))
                        if u + 2 < UNITS:
                            rope_copy(A_ROPES + n0 + u + 2, u % 2, SCALE)
                        if u >= 2:
                            output_high(u - 2)
                        if u >= 1:
                            turned_high(u - 1)
                        if u + 2 < UNITS:
                            query_high(u + 2)
                    output_high(UNITS - 2)
                    turned_high(UNITS - 1)
                    output_high(UNITS - 1)

                layernorm(hf * 2 * HT + HT)

        @block.vector
        def _(dve):
            dve.sem_inc(rope_sind, 1)
            dve.sem_inc(rope_lo, 1)
            dve.sem_inc(wide_free, 2)
            dve.sem_inc(s_read, 2)
            dve.sem_inc(pT_lo, 1)
            dve.sem_inc(o_lo, 1)
            dve.sem_inc(ln_lo, 2)
            H2 = DK // 2

            def rope_turn(n):
                dve.wait_ge(rope_in, 2 + n + 1)
                dve.tensor_tensor(rope_b[0:H2, :], rope_x[H2:DK, :], sin_t[H2:DK, :], ALU.mult)
                dve.tensor_tensor(rope_b[H2:DK, :], rope_x[0:H2, :], sin_t[0:H2, :], ALU.mult)\
                   .then_inc(rope_sind, 1)

            def rope_add(n):
                dve.wait_ge(rope_cosd, 1 + n + 1)
                dve.wait_ge(rope_sind, 1 + n + 1)
                dve.tensor_tensor(rope_a[:, :], rope_a[:, :], rope_b[:, :], ALU.add).then_inc(rope_sum, 1)

            def rope_low(n, hi, lo):
                dve.wait_ge(rope_hi, n + 1)
                dve.tensor_tensor(lo, rope_a[:, :], hi.bitcast(F32), ALU.subtract).then_inc(rope_lo, 1)

            for k in range(A_PIECES):
                c = k % C
                dst = (wk_s, wv_s)[k // C]
                dve.wait_ge(w_hi, k + 1)
                dve.tensor_tensor(dst[:, c, LO, :], raw[:, c % 2, :], dst[:, c, HI, :].bitcast(F32),
                                  ALU.subtract).then_inc(w_lo, 1)
            dve.wait_ge(tables_in, 32)
            with dve.Fori(0, NB) as b:
                steps = Steps(dve, dq_step, b * DQ_STEPS)

                def decode_codes():
                    dve.wait_ge(quant_in, 32 * (b + 1))
                    for r in range(4):
                        last = dve.tensor_scalar(spread[:, r], planes, r, 0x11111111,
                                                 ALU.logical_shift_right, ALU.bitwise_and)
                    steps.mark(last)
                    for k in range(1, BITS):
                        steps.wait()
                        steps.mark(dve.scalar_tensor_tensor(
                            nibbles, spread[:, :, k, :], k, spread[:, :, 0, :] if k == 1 else nibbles,
                            ALU.logical_shift_left, ALU.bitwise_or))
                    steps.wait()
                    place = codes.rearrange("p (w j r) -> p j r w", j=8, r=4)
                    for j in range(8):
                        last = dve.tensor_scalar(place[:, j], nibbles, 4 * j, LEVELS - 1,
                                                 ALU.logical_shift_right, ALU.bitwise_and)
                    steps.mark(last)

                def decode_level(dst, level):
                    return dve.tensor_scalar(dst, codes, float(level), lut_t[:, level:level + 1],
                                             ALU.is_equal, ALU.mult)

                def decode_pair(i):
                    if i == 0:
                        steps.wait()
                        decode_level(sum_v, 0)
                        decode_level(sum_p, 1).then_inc(term_ready, 1)
                    else:
                        steps.wait()
                        steps.mark(decode_level(term_v, 2 * i))
                        dve.wait_ge(term_used, b * (LEVELS // 2) + i)
                        decode_level(term_p, 2 * i + 1).then_inc(term_ready, 1)
                        steps.wait()
                        steps.mark(dve.tensor_tensor(sum_v, sum_v, term_v, ALU.add))

                for j in range(4):
                    dve.wait_ge(ctx_hi, 4 * b + j + 1)
                    dve.tensor_tensor(ctxT[:, 2 * j:2 * j + 2, LO, :],
                                      ctx_ps[j][:, :].rearrange("p (c n) -> p c n", c=2),
                                      ctxT[:, 2 * j:2 * j + 2, HI, :].bitcast(F32),
                                      ALU.subtract).then_inc(ctx_lo, 1)
                decode_codes()
                for g in range(HKV):
                    n = b * HKV + g
                    rope_turn(n)
                    rope_add(n)
                    rope_low(n, k_stage[:, g % 2, HI, :], k_stage[:, g % 2, LO, :])
                    decode_pair(g)
                assert steps.n == DQ_STEPS
                for t in range(TS):
                    for n in range(NN):
                        dve.wait_ge(stage_hi, b * V_USES + t * NN + n + 1)
                        dve.tensor_tensor(v_stage[:, LO, :], wide_ps[n][:, :], v_stage[:, HI, :].bitcast(F32),
                                          ALU.subtract).then_inc(stage_lo, 1)
                        if t == 0 and n == 1:
                            steps.wait()
                            dve.wait_ge(term_used, (b + 1) * (LEVELS // 2))
                            dve.tensor_tensor(sum_v, sum_v, sum_p, ALU.add).then_inc(w4_ready, 1)
                for j in range(2):
                    dve.wait_ge(stage_hi, b * V_USES + TS * NN + j + 1)
                    dve.tensor_tensor(v_stage[:, LO, :], w4_ps[j][:, :], v_stage[:, HI, :].bitcast(F32),
                                      ALU.subtract).then_inc(stage_lo, 1)

            def layernorm_stats(steps, at, t, loaded):
                s = t % 2
                if loaded is not None:
                    dve.wait_ge(x_in[t], loaded)
                for n in range(NN):
                    last = dve.bn_stats(ln_stat[:, s, n, :], acc[:, t, n * BANK:(n + 1) * BANK])
                steps.mark(last)
                steps.wait()
                hold(dve)
                steps.mark(dve.bn_aggr(ln_mv[:, s, :], ln_stat[:, s, :, :].rearrange("p n k -> p (n k)")))
                steps.wait()
                dve.tensor_scalar(ln_ve[:, s:s + 1], ln_mv[:, s, 1:2], EPS, None, ALU.add).then_inc(ln_var, 1)

            def layernorm_rows(steps, at, t):
                s = t % 2
                col = slice(s, s + 1)
                dve.wait_ge(ln_std, at + t + 1)
                steps.mark(dve.reciprocal(ln_y[:, col], ln_sd[:, col]))
                steps.wait()
                steps.mark(dve.tensor_scalar(ln_e[:, col], ln_y[:, col], ln_y[:, col], ln_ve[:, col],
                                             ALU.mult, ALU.mult))
                steps.wait()
                steps.mark(dve.tensor_scalar(ln_f[:, col], ln_e[:, col], -0.5, 1.5, ALU.mult, ALU.add))
                steps.wait()
                steps.mark(dve.tensor_tensor(ln_r[:, col], ln_y[:, col], ln_f[:, col], ALU.mult))
                steps.wait()
                dve.wait_ge(ln_tr, at + t + 1)
                dve.tensor_scalar(raw[:, s, :], acc[:, t, :], ln_mv[:, s, 0:1], ln_r[:, col],
                                  ALU.subtract, ALU.mult).then_inc(ln_rows, 1)

            def layernorm_low(at, t):
                dve.wait_ge(ln_hi, at + t + 1)
                for j in range(2):
                    part = xT[:, 4 * j:4 * j + 4, :, t * P:(t + 1) * P]
                    last = dve.tensor_tensor(part[:, :, LO, :],
                                             ln_ps[t % 2][j][:, :].rearrange("p (c n) -> p c n", c=4),
                                             part[:, :, HI, :].bitcast(F32), ALU.subtract)
                last.then_inc(ln_lo, 1)

            def layernorm(at, loaded, between=None):
                steps = Steps(dve, ln_step, at * LN_STEPS)
                layernorm_stats(steps, at, 0, loaded)
                for t in range(HT):
                    if t + 1 < HT:
                        layernorm_stats(steps, at, t + 1, loaded)
                    layernorm_rows(steps, at, t)
                    if t >= 1:
                        layernorm_low(at, t - 1)
                    if between and t >= 2:
                        between(t - 2)
                layernorm_low(at, HT - 1)
                if between:
                    between(HT - 2)
                    between(HT - 1)
                assert steps.n == HT * LN_STEPS

            with dve.Fori(0, NH) as hf:
                wide0 = A_WIDE + hf * HALF_WIDE
                dve.wait_ge(w_lo, A_PIECES + hf * HALF_PIECES + REP)
                layernorm(hf * 2 * HT, 16 * (hf + 1))

                with dve.Fori(0, HKV) as g:
                    n0 = hf * HALF_UNITS + g * UNITS
                    w0 = wide0 + g * HB * BURST

                    def add_mask(u):
                        if u % REP == 0:
                            dve.wait_ge(mask_in, 16 * (hf * HKV * HB + g * HB + u // REP + 1))
                        dve.wait_ge(pT_tr, n0 + u + 1)
                        dve.wait_ge(s_mm, 1 + n0 + u + 1)
                        hold(dve)
                        for t in range(TS):
                            last = dve.tensor_tensor_reduce(
                                out=probs[:, u % 2, t, :], in0=s_ps[u % 2][:, t * S:(t + 1) * S],
                                in1=mask_t[:, t, :], scale=1.0, scalar=-3.0e38, op0=ALU.add, op1=ALU.max,
                                accum_out=row_max[:, u % 2, t:t + 1])
                        last.then_inc(s_read, 1)
                        dve.wait_ge(s_read, 2 + n0 + u + 1)
                        dve.tensor_scalar(neg_max[:, u % 2, :], row_max[:, u % 2, :], -1.0, None,
                                          ALU.mult).then_inc(s_max, 1)

                    def invert(u):
                        dve.wait_ge(exp_done, n0 + u + 1)
                        dve.reciprocal(row_inv[:, u % 2, :], row_sum[:, u % 2, :]).then_inc(inv_ready, 1)

                    def turned_low(u):
                        dve.wait_ge(pT_hi, n0 + u + 1)
                        dve.tensor_tensor(pT_s[:, LO, :, :], pT_ps[:, :].rearrange("p (k n) -> p k n", k=TS),
                                          pT_s[:, HI, :, :].bitcast(F32), ALU.subtract).then_inc(pT_lo, 1)

                    def output_low(u):
                        h = u % REP
                        dve.wait_ge(o_hi, n0 + u + 1)
                        dve.tensor_tensor(o_s[:, h, LO, :], o_ps[:, 0:S], o_s[:, h, HI, :].bitcast(F32),
                                          ALU.subtract).then_inc(o_lo, 1)

                    def add_projection(b):
                        for t in range(TS):
                            for n in range(NN):
                                dve.wait_ge(wide_mm, w0 + b * BURST + t * NN + n + 1)
                                part = acc[:, b * TS + t, n * BANK:(n + 1) * BANK]
                                dve.tensor_tensor(part, part, wide_ps[n][:, :], ALU.add).then_inc(wide_free, 1)

                    def rope_parts(u):
                        rope_turn(A_ROPES + n0 + u)
                        rope_add(A_ROPES + n0 + u)

                    def query_low(u):
                        rope_low(A_ROPES + n0 + u, q_s[:, u % 4, HI, :], q_s[:, u % 4, LO, :])

                    for u in range(2):
                        rope_parts(u)
                        query_low(u)
                    for u in range(UNITS):
                        add_mask(u)
                        if u >= 6 and u % REP == 2:
                            add_projection(u // REP - 1)
                        if u + 2 < UNITS:
                            rope_parts(u + 2)
                        invert(u)
                        if u >= 2:
                            output_low(u - 2)
                        if u >= 1:
                            turned_low(u - 1)
                        if u + 2 < UNITS:
                            query_low(u + 2)
                    output_low(UNITS - 2)
                    turned_low(UNITS - 1)
                    output_low(UNITS - 1)
                    add_projection(HB - 1)

                def add_layer(t):
                    dve.wait_ge(biased, hf * HT + t + 1)
                    for n in range(NN):
                        dve.wait_ge(wide_mm, wide0 + HKV * HB * BURST + t * NN + n + 1)
                        part = acc[:, t, n * BANK:(n + 1) * BANK]
                        dve.tensor_tensor(part, part, wide_ps[n][:, :], ALU.add).then_inc(wide_free, 1)
                        if n == NN - 1:
                            dve.wait_ge(wide_free, 2 + wide0 - A_WIDE + HKV * HB * BURST + (t + 1) * NN)
                            dve.sem_inc(out_ready, 1)

                dve.wait_ge(wide_free, 2 + wide0 - A_WIDE + HKV * HB * BURST)
                dve.wait_ge(w_lo, A_PIECES + (hf + 1) * HALF_PIECES)
                layernorm(hf * 2 * HT + HT, None, add_layer)

        @block.gpsimd
        def _(pool):
            pool.sem_inc(rope_cosd, 1)
            for s in range(2):
                pool.sem_inc(k_stored[s], 16)
            pool.sem_inc(v_stored, 32)
            pool.memset(ident[:, :], 0.0).then_inc(ident_step, 1)
            pool.wait_ge(ident_step, 1)
            pool.affine_select(out=ident[:, :], in_=ident[:, :], compare_op=ALU.not_equal, fill=1.0, base=0,
                               pattern=[[-1, P]], channel_multiplier=1).then_inc(ident_ok, 1)

            def rope_first(n):
                pool.wait_ge(rope_lo, n + 1)
                pool.wait_ge(rope_in, 2 + n + 1)
                pool.tensor_tensor(rope_a[:, :], rope_x[:, :], cos_t[:, :], ALU.mult).then_inc(rope_cosd, 1)

            def split_lo(k, slot, hi, lo):
                pool.wait_ge(w_hi, k + 1)
                src = raw[:, slot, :]
                if len(hi.shape) == 3:
                    src = src.rearrange("p (c n) -> p c n", c=C)
                pool.tensor_tensor(lo, src, hi.bitcast(F32), ALU.subtract).then_inc(w_lo, 1)

            pool.wait_ge(tables_in, 32)
            with pool.Fori(0, NB) as b:
                for g in range(HKV):
                    rope_first(b * HKV + g)
                    pool.wait_ge(term_ready, b * (LEVELS // 2) + g + 1)
                    if g == 0:
                        pool.sem_inc(term_used, 1)
                    else:
                        pool.wait_ge(term_used, b * (LEVELS // 2) + g)
                        pool.tensor_tensor(sum_p, sum_p, term_p, ALU.add).then_inc(term_used, 1)

            with pool.Fori(0, NH) as hf:
                piece = A_PIECES + hf * HALF_PIECES
                for h in range(REP):
                    split_lo(piece + h, h % 2, wq_s[:, h, :, HI, :], wq_s[:, h, :, LO, :])

                with pool.Fori(0, HKV) as g:
                    n0 = hf * HALF_UNITS + g * UNITS
                    p0 = piece + REP + g * 2 * REP
                    rope_first(A_ROPES + n0)
                    rope_first(A_ROPES + n0 + 1)
                    for u in range(UNITS):
                        if u + 2 < UNITS:
                            rope_first(A_ROPES + n0 + u + 2)
                        pool.wait_ge(inv_ready, n0 + u + 1)
                        hold(pool)
                        for t in range(TS):
                            last = pool.tensor_scalar(probs[:, u % 2, t, :], probs[:, u % 2, t, :],
                                                      row_inv[:, u % 2, t:t + 1], 1.0, ALU.mult, ALU.mult)
                        last.then_inc(p_ready, 1)
                        if u < REP:
                            split_lo(p0 + u, u % 2, wo_s[:, u, HI, :], wo_s[:, u, LO, :])
                        if u >= UNITS - REP:
                            h = u - (UNITS - REP)
                            split_lo(p0 + REP + h, h % 2, wq_s[:, h, :, HI, :], wq_s[:, h, :, LO, :])

                pool.wait_ge(bias_in, 16 * (hf + 1))
                for t in range(HT):
                    pool.wait_ge(ln_rows, hf * 2 * HT + HT + t + 1)
                    pool.tensor_tensor(acc[:, t, :], acc[:, t, :], bias_t, ALU.add).then_inc(biased, 1)


_INS = ("x", "ctx_4096", "mask_BxSxS2_ff0", "L0_xattn_wq", "L0_xattn_wk", "L0_xattn_wv", "L0_xattn_wo",
        "L0_ffn_qweight", "L0_ffn_lut4", "L0_ffn_bias")


def _rope_tables(positions, width):
    import numpy as np

    f = np.float32
    inv = f(1.0) / np.power(f(10000.0), np.arange(0, width, 2, dtype=f) / f(width))
    angle = (np.arange(positions, dtype=f)[None, :] * inv.astype(f)[:, None]).astype(f)
    cos, sin = np.cos(angle).astype(f), np.sin(angle).astype(f)
    return np.concatenate([cos, cos]), np.concatenate([sin, -sin])


def kernel(**inputs):
    import numpy as np
    import concourse.bacc as bacc
    from concourse import mybir
    from concourse.bass_utils import run_bass_kernel_spmd

    nc = bacc.Bacc("TRN2", target_bir_lowering=False, num_devices=1)
    arrays = {name: np.ascontiguousarray(inputs[name]) for name in _INS}
    shape = arrays["x"].shape
    arrays["rope_cos"], arrays["rope_sin"] = _rope_tables(shape[1], 128)
    args = [nc.dram_tensor(f"in_{n}", a.shape, mybir.dt.from_np(a.dtype), kind="ExternalInput").ap()
            for n, a in arrays.items()]
    out = nc.dram_tensor("out_y", shape, mybir.dt.float32, kind="ExternalOutput").ap()
    build_xattn_ffn(nc, *args, out)
    r = run_bass_kernel_spmd(nc, [{f"in_{n}": a for n, a in arrays.items()}], core_ids=[0])
    return r.results[0]["out_y"]
```

```python
class Steps:

    def __init__(self, eng, sem, base):
        self.eng, self.sem, self.base, self.n = eng, sem, base, 0

    def mark(self, instruction):
        instruction.then_inc(self.sem, 1)
        self.n += 1

    def wait(self):
        self.eng.wait_ge(self.sem, self.base + self.n)


def build_xattn_ffn(nc, x, ctx, mask, wq, wk, wv, wo, qweight, lut4, bias, rope_cos, rope_sin, out):
    from contextlib import ExitStack

    from concourse import mybir

    F32, F32R, I32 = mybir.dt.float32, mybir.dt.float32r, mybir.dt.int32
    ALU, ACT = mybir.AluOpType, mybir.ActivationFunctionType

    P = 128
    NB, S, D = x.shape
    DK = P
    HQ, HKV = wq.shape[1] // DK, wk.shape[1] // DK
    REP = HQ // HKV
    C = D // P
    TS = S // P
    NH = 2
    HB = NB // NH
    HT = HB * TS
    UNITS = HB * REP
    BITS = 4
    LEVELS = 1 << BITS
    WORDS = D // 32
    BANK = 512
    NN = D // BANK
    EPS = 1e-5
    SCALE = float(DK) ** -0.5
    HI, LO = 0, 1
    PASSES = ((HI, HI), (HI, LO), (LO, HI))
    assert (S, DK, TS, NN, REP, HB, C) == (256, 128, 2, 2, 4, 4, 8)

    A_ROPES = NB * HKV
    HALF_UNITS = HKV * UNITS
    A_WIDE = 1 + NB * TS * NN
    BURST = TS * NN
    HALF_WIDE = HKV * HB * BURST + HT * NN
    A_PIECES = 2 * C
    POOL_PIECES = C // 2
    A_LOW = A_PIECES - POOL_PIECES
    HALF_PIECES = HKV * 2 * REP
    A_SLOTS = 7
    A_TURNS = 3
    V0, V1, V2, D0, D1, V3 = range(6)
    STAGED = 6
    K_TURNS = {V1: 4, D0: 5, V3: 6}
    V_TURNS = {V0: 0, V2: 1, D1: 2}
    POOL_LEVELS = 11
    CODE_STEPS = 1 + (BITS - 1) + 1
    AHEAD, LAG = 2, 3
    WO_SPLIT, WQ_SPLIT = 1, UNITS - REP - 1
    DQ_STEPS = CODE_STEPS + 1 + 2 * (LEVELS - POOL_LEVELS - 1)
    LN_LAG = 2
    LN_FIRST = HT - LN_LAG
    LN_STEPS = 2 + 4
    LN_HALF = 2 * HT
    LN_C = {}
    for t in range(HT + 1):
        if t < HT:
            LN_C[2, t] = HT + len(LN_C)
        if t - 1 >= LN_LAG:
            LN_C[1, t - 1 - LN_LAG] = HT + len(LN_C)
    assert len(LN_C) == HT + LN_FIRST

    x_tiles = x.rearrange("b (t p) d -> (b t) p d", p=P)
    out_tiles = out.rearrange("b (t p) d -> (b t) p d", p=P)
    ctx_tiles = ctx.rearrange("b (t p) d -> b t p d", p=P)
    mask_v = mask.rearrange("b (t p) k -> b p t k", p=P)
    wk_v = wk.rearrange("(c p) n -> c p n", p=P)
    wv_v = wv.rearrange("(c p) n -> c p n", p=P)
    wq_v = wq.rearrange("(c p) (h n) -> h p c n", p=P, n=DK)
    wo_v = wo.rearrange("(h p) n -> h p n", p=DK)
    qw_v = qweight[0:BITS].rearrange("k (t p) w -> t p k w", p=P)
    lut_v = lut4.rearrange("(t p) l -> t p l", p=P)
    bias_v = bias.rearrange("(a n) -> a n", a=1)
    k_scr = nc.dram_tensor("k_scratch", (HKV, NB, P, 2 * S), F32, kind="Internal").ap()
    v_scr = nc.dram_tensor("v_scratch", (NB, TS, 2, P, HKV * DK), F32, kind="Internal").ap()
    w_scr = nc.dram_tensor("w_scratch", (P, 2, C, D), F32, kind="Internal").ap()

    with ExitStack() as stack:
        def sb(name, shape, dt):
            return stack.enter_context(nc.sbuf_tensor(name, shape, dt))

        def sem(name):
            return stack.enter_context(nc.semaphore(name))

        W = sb("weights_split", [P, 2 * C * D], F32R)
        X = sb("acts_split", [P, 2 * C * D], F32R)
        R = sb("small_split", [P, 6144], F32R)
        wk_s = W[:, :].rearrange("p (c l n) -> p c l n", c=C, l=2)
        wv_s = X[:, :].rearrange("p (c l n) -> p c l n", c=C, l=2)
        ctxT = R[:, 0:4096].rearrange("p (c l n) -> p c l n", c=C, l=2)
        k_stage = R[:, 4096:5120].rearrange("p (s l n) -> p s l n", s=2, l=2)
        k_stage_all, v_stage_all = R[:, 4096:5120], R[:, 5120:6144]
        wq_s = W[:, 0:8192].rearrange("p (h c l n) -> p h c l n", h=REP, c=C, l=2)
        wo_s = W[:, 8192:16384].rearrange("p (h l n) -> p h l n", h=REP, l=2)
        xT = X[:, :].rearrange("p (c l n) -> p c l n", c=C, l=2)
        q_s = R[:, 0:2048].rearrange("p (s l n) -> p s l n", s=4, l=2)
        o_s = R[:, 2048:3072].rearrange("p (s l n) -> p s l n", s=2, l=2)
        k_s = R[:, 4096:4608].rearrange("p (l n) -> p l n", l=2)
        v_s = R[:, 4608:5120].rearrange("p (k l n) -> p k l n", k=TS, l=2)
        pT_s = R[:, 5120:6144].rearrange("p (l k n) -> p l k n", l=2, k=TS)
        w4_s = W[:, :].rearrange("p (c l n) -> p c l n", c=C, l=2)

        acc_t = sb("residual", [P, HT * D], F32)
        acc = acc_t[:, :].rearrange("p (t n) -> p t n", t=HT)
        ctx_stage = acc_t[:, 0:2048].rearrange("p (t n) -> p t n", t=TS)
        codes = acc_t[:, 2048:3072].bitcast(I32)
        term_v = acc_t[:, 3072:4096]
        sum_v = acc_t[:, 4096:5120]
        sum_p = acc_t[:, 6144:7168]
        planes = acc_t[:, 7168:7296].bitcast(I32).rearrange("p (k w) -> p k w", k=BITS)
        spread = acc_t[:, 7296:7808].bitcast(I32).rearrange("p (r k w) -> p r k w", r=4, k=BITS)
        nibbles = acc_t[:, 7808:7936].bitcast(I32).rearrange("p (r w) -> p r w", r=4)
        lut_t = acc_t[:, 7936:7936 + LEVELS]
        raw_t = sb("raw", [P, 2 * D], F32)
        raw = raw_t[:, :].rearrange("p (s n) -> p s n", s=2)
        a_raw = [raw[:, 0, :], raw[:, 1, :]] + [acc_t[:, i * D:(i + 1) * D] for i in range(2, A_SLOTS)]
        ln_row = sb("ln_row", [P, D], F32)
        term_p = [acc_t[:, 5120:6144], ln_row[:, :]]
        prob_t = sb("probs", [P, 2 * TS * S], F32)
        probs = prob_t[:, :].rearrange("p (s t k) -> p s t k", s=2, t=TS)
        bias_t = prob_t[:, :]
        mask_t = sb("mask_tile", [P, TS, S], F32)
        rope_x = sb("rope_x", [P, S], F32)
        rope_a = sb("rope_a", [P, S], F32)
        rope_b = sb("rope_b", [P, S], F32)
        ropes = [(rope_x[:, :], rope_a[:, :], rope_b[:, :]), tuple(prob_t[:, i * S:(i + 1) * S] for i in range(3))]
        cos_t = sb("cos_t", [P, S], F32)
        sin_t = sb("sin_t", [P, S], F32)
        ident = sb("ident", [P, P], F32)
        stat_t = sb("row_numbers", [P, 56], F32)
        neg_max, row_max, row_sum, row_inv = (
            stat_t[:, i * 2 * TS:(i + 1) * 2 * TS].rearrange("p (s t) -> p s t", s=2) for i in range(4))
        ln_stat = stat_t[:, 16:40].rearrange("p (s n k) -> p s n k", s=2, n=2)
        ln_mv = stat_t[:, 40:44].rearrange("p (s k) -> p s k", s=2)
        ln_ve, ln_sd, ln_y, ln_e, ln_f, ln_r = (stat_t[:, 44 + 2 * i:46 + 2 * i] for i in range(6))

        bank = [stack.enter_context(nc.psum_tensor(f"bank{i}", [P, BANK], F32)) for i in range(8)]
        ctx_ps = [bank[i] for i in (0, 1, 2, 5)]
        w4_ps = [bank[3], bank[4]]
        k_ps = [bank[3][:, 0:S], bank[4][:, 0:S]]
        q_ps = bank[3][:, 0:S]
        wide_ps = [bank[6], bank[7]]
        out_ps = [bank[1], bank[4], bank[6], bank[7]]
        s_ps = bank[0]
        pT_ps = bank[2]
        o_ps = bank[5][:, 0:S]
        ln_ps = [(bank[0], bank[3]), (bank[2], bank[5])]
        ln_ps_beside = {LN_FIRST: (bank[1], bank[4]),
                        LN_FIRST + 1: (bank[6], bank[7])}

        tables_in = sem("tables_in")
        ctx_in = [sem(f"ctx_in{t}") for t in range(TS)]
        planes_in, lut_in = sem("planes_in"), sem("lut_in")
        a_raw_in = [sem(f"raw_in{s}") for s in range(A_SLOTS)]
        raw_in = a_raw_in[0:2]
        x_in = [sem(f"x_in{t}") for t in range(HT)]
        k_in, v_in, mask_in = sem("k_in"), sem("v_in"), sem("mask_in")
        w4_in = [sem(f"w4_in{c}") for c in range(C)]
        bias_in = sem("bias_in")
        k_stored = [sem(f"k_stored{s}") for s in range(2)]
        v_stored = sem("v_stored")
        out_stored = sem("out_stored")
        ident_step, ident_ok = sem("ident_step"), sem("ident_ok")
        w_hi, w_lo, wv_lo = sem("w_hi"), sem("w_lo"), sem("wv_lo")
        ctx_tr, ctx_hi, ctx_lo = sem("ctx_tr"), sem("ctx_hi"), sem("ctx_lo")
        ctx_used = sem("ctx_used")
        stage_hi, stage_lo = sem("stage_hi"), sem("stage_lo")
        dq_step = sem("dq_step")
        term_ready, term_used = sem("term_ready"), sem("term_used")
        w4_ready, w4_tr = sem("w4_ready"), sem("w4_tr")
        rope_mm, rope_in = sem("rope_mm"), sem("rope_in")
        rope_cosd, rope_sind = sem("rope_cosd"), sem("rope_sind")
        rope_sum, rope_hi, rope_lo = sem("rope_sum"), sem("rope_hi"), sem("rope_lo")
        wide_mm, wide_free = sem("wide_mm"), sem("wide_free")
        s_mm, s_read, s_max = sem("s_mm"), sem("s_read"), sem("s_max")
        exp_done, inv_ready, inv_max = sem("exp_done"), sem("inv_ready"), sem("inv_max")
        p_ready, pT_tr, pT_hi, pT_lo = sem("p_ready"), sem("pT_tr"), sem("pT_hi"), sem("pT_lo")
        o_mm, o_hi, o_lo = sem("o_mm"), sem("o_hi"), sem("o_lo")
        ln_step, ln_var, ln_std = sem("ln_step"), sem("ln_var"), sem("ln_std")
        ln_rows, ln_tr, ln_hi, ln_lo = sem("ln_rows"), sem("ln_tr"), sem("ln_hi"), sem("ln_lo")
        biased, out_ready, w4_used = sem("biased"), sem("out_ready"), sem("w4_used")
        held = sem("held")

        def ln_banks(e):
            return ln_ps_beside.get(e, ln_ps[e % 2])

        def staging(i):
            return (k_stage_all, k_stored[0]) if i in K_TURNS else (v_stage_all, v_stored)

        def hold(eng):
            eng.sem_inc(held, 1)

        block = stack.enter_context(nc.Block())

        @block.sync
        def _(sp):
            def load_piece(src, stage, arrived):
                if len(src.shape) == 3:
                    stage = stage.rearrange("p (c n) -> p c n", c=C)
                sp.dma_start(stage, src).then_inc(arrived, 16)

            def load_raw(k, src, slot):
                sp.wait_ge(w_lo, A_LOW + k - 1)
                load_piece(src, raw[:, slot, :], raw_in[slot])

            for t in range(TS):
                sp.dma_start(ctx_stage[:, t, :], ctx_tiles[0, t]).then_inc(ctx_in[t], 16)
            for k in range(A_PIECES):
                if A_SLOTS <= k < A_SLOTS + C:
                    sp.wait_ge(w_lo, k - A_SLOTS + 1)
                elif k >= A_SLOTS + C:
                    sp.wait_ge(wv_lo, k - A_SLOTS - C + 1)
                load_piece((wk_v, wv_v)[k // C][k % C], a_raw[k % A_SLOTS], a_raw_in[k % A_SLOTS])
                if k == C - 1:
                    sp.dma_start(cos_t[:, :], rope_cos).then_inc(tables_in, 16)
                    sp.dma_start(sin_t[:, :], rope_sin).then_inc(tables_in, 16)
                    sp.dma_start(planes, qw_v[0]).then_inc(planes_in, 16)
                    sp.dma_start(lut_t, lut_v[0]).then_inc(lut_in, 16)

            def batch(b, last=False):
                if last:
                    sp.wait_ge(ctx_tr, 4 * NB)
                    for t in range(TS):
                        sp.dma_start(acc[:, t, :], x_tiles[t]).then_inc(x_in[t], 16)
                    for h in range(2):
                        load_raw(h, wq_v[h], h)
                else:
                    sp.wait_ge(ctx_tr, 4 * b + 4)
                    hold(sp)
                    for t in range(TS):
                        sp.dma_start(ctx_stage[:, t, :], ctx_tiles[b + 1, t]).then_inc(ctx_in[t], 16)
                for g in range(HKV):
                    sp.wait_ge(rope_lo, 2 + b * HKV + g + 1)
                    sp.dma_start(k_scr[g, b], k_stage[:, g % 2].bitcast(F32)
                                 .rearrange("p l n -> p (l n)")).then_inc(k_stored[g % 2], 16)
                if not last:
                    sp.dma_start(planes, qw_v[b + 1]).then_inc(planes_in, 16)

                def store_values(i, t, n):
                    sp.wait_ge(stage_lo, STAGED // 2 + b * STAGED + i + 1)
                    stage, stored = staging(i)
                    sp.dma_start(v_scr[b, t, :, :, n * BANK:(n + 1) * BANK].rearrange("l p n -> p l n"),
                                 stage.bitcast(F32).rearrange("p (l n) -> p l n", l=2)).then_inc(stored, 16)

                def store_weights(i, j):
                    sp.wait_ge(stage_lo, STAGED // 2 + b * STAGED + i + 1)
                    stage, stored = staging(i)
                    dst = w_scr.rearrange("p j k (t n) -> t j p k n", n=P)
                    sp.dma_start(dst[b, j], stage.bitcast(F32).rearrange("p (k n) -> p k n", n=P)
                                 ).then_inc(stored, 16)

                def load_rows(tiles):
                    for t in tiles:
                        sp.dma_start(acc[:, t, :], x_tiles[t]).then_inc(x_in[t], 16)

                store_values(V0, 0, 0)
                store_values(V1, 0, 1)
                store_values(V2, 1, 0)
                store_weights(D0, 0)
                if not last:
                    sp.dma_start(lut_t, lut_v[b + 1]).then_inc(lut_in, 16)
                else:
                    sp.wait_ge(w4_tr, 2 * NB)
                    load_rows((2, 3))
                    load_raw(2, wq_v[2], 0)
                store_weights(D1, 1)
                if last:
                    load_rows((4,))
                    load_raw(3, wq_v[3], 1)
                store_values(V3, 1, 1)
                if last:
                    load_rows(range(5, HT))

            with sp.Fori(0, NB - 1) as b:
                batch(b)
            batch(NB - 1, last=True)
            sp.wait_ge(k_stored[0], 16 + 16 * NB * (HKV // 2 + len(K_TURNS)))
            sp.wait_ge(k_stored[1], 16 + 16 * NB * (HKV // 2))
            sp.wait_ge(v_stored, 16 + 16 * NB * len(V_TURNS))

            with sp.Fori(0, NH) as hf:
                other = sp.snap((hf + 1) % NH)
                piece = hf * HALF_PIECES

                def load_step(g, last):
                    n0 = hf * HALF_UNITS + g * UNITS
                    for b in range(HB):
                        batch = hf * HB + b
                        n = n0 + b * REP

                        def load_values():
                            sp.wait_ge(o_mm, n + 1)
                            hold(sp)
                            v_src = v_scr[batch].rearrange("k l p (g n) -> g p (k l) n", n=DK)
                            sp.dma_start(v_s.bitcast(F32).rearrange("p k l n -> p (k l) n"),
                                         v_src[g]).then_inc(v_in, 16)

                        sp.wait_ge(s_mm, n + 1)
                        hold(sp)
                        sp.dma_start(k_s.bitcast(F32).rearrange("p l n -> p (l n)"),
                                     k_scr[g, batch]).then_inc(k_in, 16)
                        sp.wait_ge(s_read, n + 1)
                        hold(sp)
                        sp.dma_start(mask_t[:, :, :], mask_v[batch]).then_inc(mask_in, 16)
                        for h in range(REP):
                            if b == 0:
                                if h == 2:
                                    load_values()
                                load_raw(piece + REP + g * 2 * REP + h, wo_v[g * REP + h], h % 2)
                        if b in (1, 2):
                            load_values()
                        if b >= 2 and not last:
                            for h in (2 * b - 4, 2 * b - 3):
                                load_raw(piece + 2 * REP + g * 2 * REP + h, wq_v[(g + 1) * REP + h], h % 2)
                        if b == HB - 1:
                            load_values()
                with sp.Fori(0, HKV - 1) as g:
                    load_step(g, False)
                load_step(HKV - 1, True)
                units = (hf + 1) * HALF_UNITS
                for c in range(C):
                    if c == 0:
                        sp.wait_ge(rope_mm, A_ROPES + units)
                    elif c == REP:
                        sp.wait_ge(o_mm, 1 + units - 1)
                    elif c == REP + 1:
                        sp.wait_ge(o_mm, 1 + units)
                    elif c == REP + 2:
                        sp.wait_ge(wide_mm, A_WIDE + hf * HALF_WIDE + HKV * HB * BURST)
                    hold(sp)
                    w4_src = w_scr.rearrange("p j (l c) n -> j c p l n", l=2)
                    sp.dma_start(w4_s[:, c].bitcast(F32), w4_src[c // 4, c % 4]).then_inc(w4_in[c], 16)
                    if c == REP + 1:
                        sp.wait_ge(pT_tr, 2 + units)
                        sp.dma_start(bias_t, bias_v.to_broadcast([P, D])).then_inc(bias_in, 16)
                for h in range(2):
                    load_raw(piece + HALF_PIECES + h, wq_v[h], h)
                for t in range(HT):
                    sp.wait_ge(out_ready, hf * HT + t + 1)
                    hold(sp)
                    sp.dma_start(out_tiles[hf * HT + t], acc[:, t, :]).then_inc(out_stored, 16)
                    sp.wait_ge(out_stored, 16 * (hf * HT + t + 1))
                    hold(sp)
                    sp.dma_start(acc[:, t, :], x_tiles[other * HT + t]).then_inc(x_in[t], 16)
                    if t == HT - 2:
                        for h in range(2, REP):
                            load_raw(piece + HALF_PIECES + h, wq_v[h], h % 2)
            for t in range(HT):
                sp.wait_ge(x_in[t], 16 * (NH + 1))

        @block.tensor
        def _(pe):
            pe.sem_inc(s_mm, 1)
            pe.sem_inc(o_mm, 1)
            pe.sem_inc(pT_tr, 2)
            pe.sem_inc(ln_tr, 1)
            pe.sem_inc(wide_mm, 1)
            pe.wait_ge(ident_ok, 1)

            def turn_context(loaded):
                for t in range(TS):
                    pe.wait_ge(ctx_in[t], loaded)
                    for c in range(C):
                        col = (c % 2) * S + t * P
                        last = pe.transpose(ctx_ps[c // 2][:, col:col + P],
                                            ctx_stage[:, t, c * P:(c + 1) * P], ident[:, :])
                        if t == TS - 1 and c % 2:
                            last.then_inc(ctx_tr, 1)

            turn_context(16)

            def batch(b, last=False):
                for g in range(HKV):
                    if g < 2:
                        pe.wait_ge(stage_lo, b * STAGED + g + 1)
                    pe.wait_ge(rope_in, b * HKV + g + 1)
                    for c in range(C):
                        if g == 0:
                            pe.wait_ge(w_lo, c + 1)
                            pe.wait_ge(ctx_lo, 4 * b + c // 2 + 1)
                        for i, (a, m) in enumerate(PASSES):
                            done = pe.matmul(k_ps[g % 2], wk_s[:, c, a, g * DK:(g + 1) * DK],
                                             ctxT[:, c, m, :], start=c == 0 and i == 0,
                                             stop=c == C - 1 and i == 2)
                    done.then_inc(rope_mm, 1)

                def values(t, n, split):
                    pe.wait_ge(stage_lo, split)
                    for c in range(C):
                        for i, (a, m) in enumerate(PASSES):
                            done = pe.matmul(wide_ps[n][:, :], ctxT[:, c, a, t * P:(t + 1) * P],
                                             wv_s[:, c, m, n * BANK:(n + 1) * BANK],
                                             start=c == 0 and i == 0, stop=c == C - 1 and i == 2)
                        if not last and t == TS - 1 and n == NN - 1 and c in (1, 3, 5):
                            done.then_inc(ctx_used, 1)
                    done.then_inc(wide_mm, 1)

                pe.wait_ge(w_lo, A_LOW)
                pe.wait_ge(wv_lo, POOL_PIECES)
                values(0, 0, 2 + b * STAGED)
                values(0, 1, STAGED // 2 + b * STAGED)
                values(1, 0, STAGED // 2 + b * STAGED + V0 + 1)
                if not last:
                    turn_context(16 * (b + 2))
                pe.wait_ge(rope_in, 2 + (b + 1) * HKV)
                pe.wait_ge(w4_ready, b + 1)
                for c in range(C):
                    done = pe.transpose(w4_ps[c // 4][:, (c % 4) * P:(c % 4 + 1) * P],
                                        sum_v[:, c * P:(c + 1) * P], ident[:, :])
                    if c % 4 == 3:
                        done.then_inc(w4_tr, 1)
                values(1, 1, STAGED // 2 + b * STAGED + V1 + 1)

            with pe.Fori(0, NB - 1) as b:
                batch(b)
            batch(NB - 1, last=True)

            def turn_rows(base, e):
                pe.wait_ge(ln_rows, base + e + 1)
                pe.wait_ge(ln_lo, base + e + 1)
                for c in range(C):
                    last = pe.transpose(ln_banks(e)[c // 4][:, (c % 4) * P:(c % 4 + 1) * P],
                                        ln_row[:, c * P:(c + 1) * P], ident[:, :])
                last.then_inc(ln_tr, 1)

            for e in range(LN_FIRST):
                turn_rows(0, e)
            with pe.Fori(0, NH) as hf:
                piece = A_LOW + hf * HALF_PIECES
                wide0 = A_WIDE + hf * HALF_WIDE
                ln0 = hf * LN_HALF

                def query(r, wanted, u):
                    b, h = u // REP % HB, u % REP
                    if b == 0:
                        pe.wait_ge(w_lo, wanted)
                    if b == HB - 1 and h == 0:
                        pe.wait_ge(ln_lo, 2 + ln0 + HT)
                    pe.wait_ge(rope_in, 2 + r)
                    for c in range(C):
                        for i, (a, m) in enumerate(PASSES):
                            last = pe.matmul(q_ps, wq_s[:, h, c, a, :],
                                             xT[:, c, m, b * S:(b + 1) * S],
                                             start=c == 0 and i == 0, stop=c == C - 1 and i == 2)
                    last.then_inc(rope_mm, 1)

                r_half = A_ROPES + hf * HALF_UNITS
                pe.wait_ge(ln_lo, 2 + ln0 + LN_FIRST)
                query(r_half, piece + 1, 0)
                query(r_half + 1, piece + 2, 1)
                turn_rows(ln0, LN_FIRST)

                def step(g, units, last=False):
                    n0 = hf * HALF_UNITS + g * UNITS
                    w0 = wide0 + g * HB * BURST
                    r0 = r_half + g * UNITS

                    def scores(u):
                        if u % REP == 0:
                            pe.wait_ge(k_in, 16 * (hf * HKV * HB + g * HB + u // REP + 1))
                        pe.wait_ge(rope_lo, 2 + r0 + u + 1)
                        pe.wait_ge(s_read, n0 + u + 1)
                        for t in range(TS):
                            for i, (a, m) in enumerate(PASSES):
                                last = pe.matmul(s_ps[:, t * S:(t + 1) * S],
                                                 q_s[:, u % 4, a, t * P:(t + 1) * P], k_s[:, m, :],
                                                 start=i == 0, stop=i == 2)
                        last.then_inc(s_mm, 1)

                    def turn(u):
                        pe.wait_ge(p_ready, n0 + u + 1)
                        pe.wait_ge(pT_lo, n0 + u + 1)
                        for t in range(TS):
                            for k in range(TS):
                                last = pe.transpose(pT_ps[:, k * S + t * P:k * S + (t + 1) * P],
                                                    probs[:, u % 2, t, k * P:(k + 1) * P], ident[:, :])
                        last.then_inc(pT_tr, 1)

                    def attend(u):
                        if u % REP == 0:
                            pe.wait_ge(v_in, 16 * (hf * HKV * HB + g * HB + u // REP + 1))
                        pe.wait_ge(pT_lo, 1 + n0 + u + 1)
                        pe.wait_ge(o_lo, n0 + u + 1)
                        for k in range(TS):
                            for i, (a, m) in enumerate(PASSES):
                                last = pe.matmul(o_ps, v_s[:, k, a, :], pT_s[:, m, k, :],
                                                 start=k == 0 and i == 0, stop=k == TS - 1 and i == 2)
                        last.then_inc(o_mm, 1)

                    def project(u):
                        b, h = u // REP, u % REP
                        if b == 0:
                            pe.wait_ge(w_lo, piece + REP + g * 2 * REP + h + 1)
                            pe.wait_ge(ln_lo, 2 + ln0 + HT)
                        pe.wait_ge(o_lo, 1 + n0 + u + 1)
                        for part in range(BURST):
                            t, n = part // NN, part % NN
                            if h == 0:
                                pe.wait_ge(wide_free, w0 - A_WIDE + b * BURST + part + 1)
                            for i, (a, m) in enumerate(PASSES):
                                last = pe.matmul(out_ps[part][:, :], o_s[:, u % 2, a, t * P:(t + 1) * P],
                                                 wo_s[:, h, m, n * BANK:(n + 1) * BANK],
                                                 start=h == 0 and i == 0, stop=h == REP - 1 and i == 2)
                            if h == REP - 1:
                                last.then_inc(wide_mm, 1)

                    for u in units:
                        if not last or u < UNITS:
                            scores(u)
                        if not last or u + AHEAD < UNITS:
                            v = u + AHEAD
                            query(r0 + v, piece + (g + v // UNITS) * 2 * REP + v % REP + 1, v)
                        if u >= 2 and (not last or u - 2 < UNITS):
                            attend(u - 2)
                        if u >= 1 and (not last or u - 1 < UNITS):
                            turn(u - 1)
                        if last and u == UNITS:
                            turn_rows(ln0, LN_C[2, 0])
                        if u >= LAG:
                            project(u - LAG)

                step(0, range(LAG - 1))
                turn_rows(ln0, LN_FIRST + 1)
                step(0, range(LAG - 1, LAG))
                with pe.Fori(0, HKV - 1) as g:
                    step(g, range(LAG, UNITS + LAG))
                step(HKV - 1, range(LAG, UNITS + LAG), last=True)

                wide_c = wide0 + HKV * HB * BURST
                for t in range(HT):
                    pe.wait_ge(ln_lo, 2 + ln0 + LN_C[2, t] + 1)
                    for n in range(NN):
                        pe.wait_ge(wide_free, wide_c - A_WIDE + t * NN + n + 1)
                    for c in range(C):
                        if t == 0:
                            pe.wait_ge(w4_in[c], 16 * (hf + 1))
                        for n in range(NN):
                            for i, (a, m) in enumerate(PASSES):
                                last = pe.matmul(out_ps[t % 2 * NN + n][:, :], xT[:, c, a, t * P:(t + 1) * P],
                                                 w4_s[:, c, m, n * BANK:(n + 1) * BANK],
                                                 start=c == 0 and i == 0, stop=c == C - 1 and i == 2)
                            if c == C - 1:
                                last.then_inc(wide_mm, 1)
                        if t == HT - 1 and c < REP:
                            last.then_inc(w4_used, 1)
                        if c == C // 2 - 1 and t + 1 < HT:
                            turn_rows(ln0, LN_C[2, t + 1])
                    if t >= LN_LAG:
                        turn_rows(ln0, LN_C[1, t - LN_LAG])

        @block.scalar
        def _(act):
            act.sem_inc(rope_in, 2)

            def split_hi(stage, arrived, count, dst):
                act.wait_ge(arrived, 16 * count)
                if len(dst.shape) == 3:
                    stage = stage.rearrange("p (c n) -> p c n", c=C)
                act.activation(dst, stage, ACT.Copy).then_inc(w_hi, 1)

            def rope_copy(n, product, scale, slot=0, slots=1):
                act.wait_ge(rope_cosd, 2 + n - slots + 1)
                act.wait_ge(rope_sind, 2 + n - slots + 1)
                act.wait_ge(rope_mm, n + 1)
                act.activation(ropes[slot][0], product, ACT.Copy, scale=scale).then_inc(rope_in, 1)

            def rope_high(n, dst, slot=0):
                act.wait_ge(rope_sum, n + 1)
                act.activation(dst, ropes[slot][1], ACT.Copy).then_inc(rope_hi, 1)

            def context_high(first, j):
                act.wait_ge(ctx_tr, first + j + 1)
                act.activation(ctxT[:, 2 * j:2 * j + 2, HI, :], ctx_ps[j][:, :].rearrange("p (c n) -> p c n", c=2),
                               ACT.Copy).then_inc(ctx_hi, 1)

            def row_std(base, e):
                act.wait_ge(ln_var, base + e + 1)
                act.activation(ln_sd[:, e % 2:e % 2 + 1], ln_ve[:, e % 2:e % 2 + 1], ACT.Sqrt).then_inc(ln_std, 1)

            def row_high(base, e, t):
                act.wait_ge(ln_tr, 1 + base + e + 1)
                for j in range(2):
                    last = act.activation(xT[:, 4 * j:4 * j + 4, HI, t * P:(t + 1) * P],
                                          ln_banks(e)[j][:, :].rearrange("p (c n) -> p c n", c=4), ACT.Copy)
                last.then_inc(ln_hi, 1)

            for j in range(4):
                context_high(0, j)
            for k in range(A_PIECES):
                split_hi(a_raw[k % A_SLOTS], a_raw_in[k % A_SLOTS], k // A_SLOTS + 1,
                         (wk_s, wv_s)[k // C][:, k % C, HI, :])

            def batch(b, last=False):
                rope_copy(b * HKV, k_ps[0], 1.0, 0, 2)
                for g in range(HKV):
                    if g + 1 < HKV:
                        rope_copy(b * HKV + g + 1, k_ps[(g + 1) % 2], 1.0, (g + 1) % 2, 2)
                    stored = b * (HKV // 2 + (0 if g % 2 else len(K_TURNS))) + g // 2 + 1
                    act.wait_ge(k_stored[g % 2], 16 * stored)
                    rope_high(b * HKV + g, k_stage[:, g % 2, HI, :], g % 2)

                def staged_high(i, src):
                    if i in K_TURNS:
                        act.wait_ge(k_stored[0], 16 * (b * (HKV // 2 + len(K_TURNS)) + K_TURNS[i] + 1))
                    else:
                        act.wait_ge(v_stored, 16 * (b * len(V_TURNS) + V_TURNS[i] + 1))
                    act.activation(staging(i)[0][:, 0:BANK], src[:, :], ACT.Copy).then_inc(stage_hi, 1)

                def values_high(i, part):
                    act.wait_ge(wide_mm, 1 + b * TS * NN + part + 1)
                    staged_high(i, wide_ps[part % 2])

                def weights_high(i, j):
                    act.wait_ge(w4_tr, b * 2 + j + 1)
                    staged_high(i, w4_ps[j])

                def next_context_high(j):
                    if j < 3:
                        act.wait_ge(ctx_used, 3 * b + j + 1)
                    else:
                        act.wait_ge(wide_mm, 1 + (b + 1) * TS * NN)
                    context_high(4 * (b + 1), j)

                values_high(V0, 0)
                act.wait_ge(k_stored[1], 16 * (b * (HKV // 2) + HKV // 2 + 1))
                values_high(V1, 1)
                if last:
                    for h in range(2):
                        split_hi(raw[:, h, :], raw_in[h], A_TURNS + 1, wq_s[:, h, :, HI, :])
                values_high(V2, 2)
                weights_high(D0, 0)
                if not last:
                    next_context_high(0)
                weights_high(D1, 1)
                if not last:
                    for j in range(1, 4):
                        next_context_high(j)
                else:
                    row_std(0, 0)
                    row_std(0, 1)
                values_high(V3, 3)

            with act.Fori(0, NB - 1) as b:
                batch(b)
            batch(NB - 1, last=True)

            for e in range(LN_FIRST):
                row_high(0, e, e)
                if e + 2 < LN_FIRST:
                    row_std(0, e + 2)
                if e < 2:
                    h = 2 + e
                    split_hi(raw[:, e, :], raw_in[e], A_TURNS + 2, wq_s[:, h, :, HI, :])
            with act.Fori(0, NH) as hf:
                seen = A_TURNS + hf * (HALF_PIECES // 2)
                wide0 = A_WIDE + hf * HALF_WIDE
                ln0 = hf * LN_HALF
                r_half = A_ROPES + hf * HALF_UNITS
                rope_copy(r_half, q_ps, SCALE)
                row_std(ln0, LN_FIRST)
                rope_high(r_half, q_s[:, 0, HI, :])
                rope_copy(r_half + 1, q_ps, SCALE)
                rope_high(r_half + 1, q_s[:, 1, HI, :])
                row_high(ln0, LN_FIRST, LN_FIRST)

                def step(g, units, last=False):
                    n0 = hf * HALF_UNITS + g * UNITS
                    r0 = r_half + g * UNITS
                    p0 = seen + REP // 2 + g * REP

                    def exponent(u):
                        act.wait_ge(s_max, n0 + u + 1)
                        for t in range(TS):
                            last = act.activation(probs[:, u % 2, t, :], probs[:, u % 2, t, :], ACT.Exp,
                                                  bias=neg_max[:, u % 2, t:t + 1],
                                                  accum_out=row_sum[:, u % 2, t:t + 1])
                        last.then_inc(exp_done, 1)

                    def turned_high(u):
                        act.wait_ge(o_mm, n0 + u + 1)
                        act.wait_ge(pT_tr, 2 + n0 + u + 1)
                        act.activation(pT_s[:, HI, :, :], pT_ps[:, :].rearrange("p (k n) -> p k n", k=TS),
                                       ACT.Copy).then_inc(pT_hi, 1)

                    def output_high(u):
                        act.wait_ge(o_mm, 1 + n0 + u + 1)
                        act.activation(o_s[:, u % 2, HI, :], o_ps, ACT.Copy).then_inc(o_hi, 1)

                    for u in units:
                        if not last or u < UNITS:
                            exponent(u)
                        if not last or u + AHEAD < UNITS:
                            rope_copy(r0 + u + AHEAD, q_ps, SCALE)
                        if u >= 2 and (not last or u - 2 < UNITS):
                            output_high(u - 2)
                        if u >= 1 and (not last or u - 1 < UNITS):
                            turned_high(u - 1)
                        if not last or u + AHEAD < UNITS:
                            rope_high(r0 + u + AHEAD, q_s[:, (u + AHEAD) % 4, HI, :])
                        if last and u == UNITS - 4:
                            row_std(ln0, LN_C[2, 0])
                        if last and u == UNITS:
                            row_high(ln0, LN_C[2, 0], 0)
                            row_std(ln0, LN_C[2, 1])
                        h = (u - WO_SPLIT) % UNITS
                        if h < REP and (not last or u < UNITS):
                            split_hi(raw[:, h % 2, :], raw_in[h % 2],
                                     p0 + (u - WO_SPLIT) // UNITS * REP + h // 2 + 1, wo_s[:, h, HI, :])
                        h = u - WQ_SPLIT
                        if h in range(REP) and not last:
                            split_hi(raw[:, h % 2, :], raw_in[h % 2], p0 + REP // 2 + h // 2 + 1,
                                     wq_s[:, h, :, HI, :])

                step(0, range(1))
                row_std(ln0, LN_FIRST + 1)
                step(0, range(1, LAG - 1))
                row_high(ln0, LN_FIRST + 1, LN_FIRST + 1)
                step(0, range(LAG - 1, LAG))
                with act.Fori(0, HKV - 1) as g:
                    step(g, range(LAG, UNITS + LAG))
                step(HKV - 1, range(LAG, UNITS + LAG), last=True)

                for t in range(HT):
                    o = t - LN_LAG
                    if o >= 0:
                        row_std(ln0, LN_C[1, o])
                    if t + 1 < HT:
                        row_high(ln0, LN_C[2, t + 1], t + 1)
                    if t + 2 < HT:
                        row_std(ln0, LN_C[2, t + 2])
                    if t == HT - 1:
                        for h in range(REP):
                            act.wait_ge(w4_used, hf * REP + h + 1)
                            split_hi(raw[:, h % 2, :], raw_in[h % 2], seen + HALF_PIECES // 2 + h // 2 + 1,
                                     wq_s[:, h, :, HI, :])
                    if o >= 0:
                        row_high(ln0, LN_C[1, o], o)

        @block.vector
        def _(dve):
            dve.sem_inc(rope_sind, 2)
            dve.sem_inc(rope_lo, 2)
            dve.sem_inc(wide_free, BURST)
            dve.sem_inc(s_read, 1)
            dve.sem_inc(pT_lo, 1)
            dve.sem_inc(o_lo, 1)
            dve.sem_inc(ln_lo, 2)
            dve.sem_inc(stage_lo, STAGED // 2)
            H2 = DK // 2

            def rope_turn(n, slot=0):
                src, _, dst = ropes[slot]
                dve.wait_ge(rope_in, 2 + n + 1)
                dve.tensor_tensor(dst[0:H2], src[H2:DK], sin_t[H2:DK, :], ALU.mult)
                dve.tensor_tensor(dst[H2:DK], src[0:H2], sin_t[0:H2, :], ALU.mult).then_inc(rope_sind, 1)

            def rope_add(n, slot=0):
                _, total, second = ropes[slot]
                dve.wait_ge(rope_cosd, 2 + n + 1)
                dve.wait_ge(rope_sind, 2 + n + 1)
                dve.tensor_tensor(total, total, second, ALU.add).then_inc(rope_sum, 1)

            def rope_low(n, parts, slot=0):
                dve.wait_ge(rope_hi, n + 1)
                dve.tensor_tensor(parts[:, LO, :], ropes[slot][1], parts[:, HI, :].bitcast(F32),
                                  ALU.subtract).then_inc(rope_lo, 1)

            def context_low(first, j):
                dve.wait_ge(ctx_hi, first + j + 1)
                dve.tensor_tensor(ctxT[:, 2 * j:2 * j + 2, LO, :],
                                  ctx_ps[j][:, :].rearrange("p (c n) -> p c n", c=2),
                                  ctxT[:, 2 * j:2 * j + 2, HI, :].bitcast(F32),
                                  ALU.subtract).then_inc(ctx_lo, 1)

            def decode_codes(steps, loaded):
                dve.wait_ge(planes_in, loaded)
                for r in range(4):
                    last = dve.tensor_scalar(spread[:, r], planes, r, 0x11111111,
                                             ALU.logical_shift_right, ALU.bitwise_and)
                steps.mark(last)
                for k in range(1, BITS):
                    steps.wait()
                    steps.mark(dve.scalar_tensor_tensor(
                        nibbles, spread[:, :, k, :], k, spread[:, :, 0, :] if k == 1 else nibbles,
                        ALU.logical_shift_left, ALU.bitwise_or))
                steps.wait()
                place = codes.rearrange("p (w j r) -> p j r w", j=8, r=4)
                for j in range(8):
                    last = dve.tensor_scalar(place[:, j], nibbles, 4 * j, LEVELS - 1,
                                             ALU.logical_shift_right, ALU.bitwise_and)
                steps.mark(last)

            def row_stats(steps, e, t, loaded=None):
                s = e % 2
                if loaded is not None:
                    dve.wait_ge(x_in[t], loaded)
                for n in range(NN):
                    last = dve.bn_stats(ln_stat[:, s, n, :], acc[:, t, n * BANK:(n + 1) * BANK])
                steps.mark(last)
                steps.wait()
                hold(dve)
                steps.mark(dve.bn_aggr(ln_mv[:, s, :], ln_stat[:, s, :, :].rearrange("p n k -> p (n k)")))
                steps.wait()
                dve.tensor_scalar(ln_ve[:, s:s + 1], ln_mv[:, s, 1:2], EPS, None, ALU.add).then_inc(ln_var, 1)

            def rows(steps, base, e, t):
                s = e % 2
                col = slice(s, s + 1)
                dve.wait_ge(ln_std, base + e + 1)
                steps.mark(dve.reciprocal(ln_y[:, col], ln_sd[:, col]))
                steps.wait()
                steps.mark(dve.tensor_scalar(ln_e[:, col], ln_y[:, col], ln_y[:, col], ln_ve[:, col],
                                             ALU.mult, ALU.mult))
                steps.wait()
                steps.mark(dve.tensor_scalar(ln_f[:, col], ln_e[:, col], -0.5, 1.5, ALU.mult, ALU.add))
                steps.wait()
                steps.mark(dve.tensor_tensor(ln_r[:, col], ln_y[:, col], ln_f[:, col], ALU.mult))
                steps.wait()
                dve.wait_ge(ln_tr, base + e + 1)
                dve.tensor_scalar(ln_row[:, :], acc[:, t, :], ln_mv[:, s, 0:1], ln_r[:, col],
                                  ALU.subtract, ALU.mult).then_inc(ln_rows, 1)

            def row_low(base, e, t):
                dve.wait_ge(ln_hi, base + e + 1)
                for j in range(2):
                    part = xT[:, 4 * j:4 * j + 4, :, t * P:(t + 1) * P]
                    last = dve.tensor_tensor(part[:, :, LO, :],
                                             ln_banks(e)[j][:, :].rearrange("p (c n) -> p c n", c=4),
                                             part[:, :, HI, :].bitcast(F32), ALU.subtract)
                last.then_inc(ln_lo, 1)

            for j in range(4):
                context_low(0, j)
            for k in range(A_PIECES):
                if C <= k < C + POOL_PIECES:
                    continue
                parts = (wk_s, wv_s)[k // C][:, k % C]
                dve.wait_ge(w_hi, k + 1)
                dve.tensor_tensor(parts[:, LO, :], a_raw[k % A_SLOTS], parts[:, HI, :].bitcast(F32),
                                  ALU.subtract).then_inc(w_lo, 1)
            dve.wait_ge(wv_lo, POOL_PIECES)
            decode_codes(Steps(dve, dq_step, 0), 16)
            dve.wait_ge(tables_in, 32)

            def batch(b, last=False):
                steps = Steps(dve, dq_step, CODE_STEPS + b * DQ_STEPS)

                def level_term(dst, level):
                    return dve.tensor_scalar(dst, codes, float(level), lut_t[:, level:level + 1],
                                             ALU.is_equal, ALU.mult)

                def pool_term(i):
                    if i >= 3:
                        dve.wait_ge(term_used, b * POOL_LEVELS + i - 1)
                    level_term(term_p[i % 2] if i else sum_p, i).then_inc(term_ready, 1)

                def vector_term(i):
                    if i == 0:
                        steps.mark(level_term(sum_v, POOL_LEVELS))
                    else:
                        steps.wait()
                        steps.mark(level_term(term_v, POOL_LEVELS + i))
                        steps.wait()
                        steps.mark(dve.tensor_tensor(sum_v, sum_v, term_v, ALU.add))

                def staged_low(i, src):
                    stage = staging(i)[0]
                    dve.wait_ge(stage_hi, b * STAGED + i + 1)
                    dve.tensor_tensor(stage[:, BANK:2 * BANK], src[:, :], stage[:, 0:BANK].bitcast(F32),
                                      ALU.subtract).then_inc(stage_lo, 1)

                dve.wait_ge(lut_in, 16 * (b + 1))
                steps.wait()
                beside = ((0, 1), (2,), (3,), (), (4,), (5,), (), (6,))
                for g in range(HKV):
                    rope_turn(b * HKV + g, g % 2)
                    if g:
                        rope_low(b * HKV + g - 1, k_stage[:, (g - 1) % 2], (g - 1) % 2)
                    rope_add(b * HKV + g, g % 2)
                    for i in beside[g]:
                        pool_term(i)
                    if g in (3, 6):
                        vector_term(g // 3 - 1)
                rope_low(b * HKV + HKV - 1, k_stage[:, (HKV - 1) % 2], (HKV - 1) % 2)
                vector_term(2)
                pool_term(7)
                pool_term(8)
                staged_low(V0, wide_ps[0])
                vector_term(3)
                pool_term(9)
                vector_term(4)
                pool_term(10)
                staged_low(V1, wide_ps[1])
                steps.wait()
                dve.wait_ge(term_used, (b + 1) * POOL_LEVELS)
                dve.tensor_tensor(sum_v, sum_v, sum_p, ALU.add).then_inc(w4_ready, 1)
                staged_low(V2, wide_ps[0])
                staged_low(D0, w4_ps[0])
                if not last:
                    context_low(4 * (b + 1), 0)
                staged_low(D1, w4_ps[1])
                if not last:
                    for j in range(1, 4):
                        context_low(4 * (b + 1), j)
                else:
                    row_stats(ln_steps, 0, 0, 16)
                    rows(ln_steps, 0, 0, 0)
                    row_stats(ln_steps, 1, 1, 16)
                staged_low(V3, wide_ps[1])
                if not last:
                    decode_codes(steps, 16 * (b + 2))
                    assert steps.n == DQ_STEPS

            ln_steps = Steps(dve, ln_step, 0)
            with dve.Fori(0, NB - 1) as b:
                batch(b)
            batch(NB - 1, last=True)

            for e in range(LN_FIRST):
                if e + 1 < LN_FIRST:
                    rows(ln_steps, 0, e + 1, e + 1)
                if e + 2 < LN_FIRST:
                    row_stats(ln_steps, e + 2, e + 2, 16)
                row_low(0, e, e)
            with dve.Fori(0, NH) as hf:
                wide0 = A_WIDE + hf * HALF_WIDE
                ln0 = hf * LN_HALF
                r_half = A_ROPES + hf * HALF_UNITS
                steps = Steps(dve, ln_step, (ln0 + LN_FIRST) * LN_STEPS)
                rope_turn(r_half)
                row_stats(steps, LN_FIRST, LN_FIRST, 16 * (hf + 1))
                rope_add(r_half)
                rope_low(r_half, q_s[:, 0])
                rows(steps, ln0, LN_FIRST, LN_FIRST)
                rope_turn(r_half + 1)
                rope_add(r_half + 1)
                rope_low(r_half + 1, q_s[:, 1])
                row_low(ln0, LN_FIRST, LN_FIRST)

                def step(g, units, last=False):
                    n0 = hf * HALF_UNITS + g * UNITS
                    w0 = wide0 + g * HB * BURST
                    r0 = r_half + g * UNITS

                    def add_mask(u):
                        if u % REP == 0:
                            dve.wait_ge(mask_in, 16 * (hf * HKV * HB + g * HB + u // REP + 1))
                        dve.wait_ge(pT_tr, n0 + u + 1)
                        dve.wait_ge(s_mm, 1 + n0 + u + 1)
                        hold(dve)
                        for t in range(TS):
                            last = dve.tensor_tensor_reduce(
                                out=probs[:, u % 2, t, :], in0=s_ps[:, t * S:(t + 1) * S],
                                in1=mask_t[:, t, :], scale=1.0, scalar=-3.0e38, op0=ALU.add, op1=ALU.max,
                                accum_out=row_max[:, u % 2, t:t + 1])
                        last.then_inc(s_read, 1)
                        dve.wait_ge(s_read, 1 + n0 + u + 1)
                        dve.tensor_scalar(neg_max[:, u % 2, :], row_max[:, u % 2, :], -1.0, None,
                                          ALU.mult).then_inc(s_max, 1)

                    def invert(u):
                        dve.wait_ge(exp_done, n0 + u + 1)
                        dve.reciprocal(row_inv[:, u % 2, :], row_sum[:, u % 2, :]).then_inc(inv_ready, 1)

                    def turned_low(u):
                        dve.wait_ge(pT_hi, n0 + u + 1)
                        dve.tensor_tensor(pT_s[:, LO, :, :], pT_ps[:, :].rearrange("p (k n) -> p k n", k=TS),
                                          pT_s[:, HI, :, :].bitcast(F32), ALU.subtract).then_inc(pT_lo, 1)

                    def output_low(u):
                        dve.wait_ge(o_hi, n0 + u + 1)
                        dve.tensor_tensor(o_s[:, u % 2, LO, :], o_ps, o_s[:, u % 2, HI, :].bitcast(F32),
                                          ALU.subtract).then_inc(o_lo, 1)

                    def add_projection(b):
                        for t in range(TS):
                            for n in range(NN):
                                dve.wait_ge(wide_mm, w0 + b * BURST + t * NN + n + 1)
                                part = acc[:, b * TS + t, n * BANK:(n + 1) * BANK]
                                dve.tensor_tensor(part, part, out_ps[t * NN + n][:, :],
                                                  ALU.add).then_inc(wide_free, 1)

                    for u in units:
                        if not last or u < UNITS:
                            add_mask(u)
                            invert(u)
                        if not last or u + AHEAD < UNITS:
                            rope_turn(r0 + u + AHEAD)
                        if u >= 2 and (not last or u - 2 < UNITS):
                            output_low(u - 2)
                        if u >= 1 and (not last or u - 1 < UNITS):
                            turned_low(u - 1)
                        if not last or u + AHEAD < UNITS:
                            rope_add(r0 + u + AHEAD)
                            rope_low(r0 + u + AHEAD, q_s[:, (u + AHEAD) % 4])
                        if u >= LAG and (u - LAG) % REP == REP - 1:
                            add_projection((u - LAG) // REP)
                        if last and u == UNITS - 4:
                            row_stats(steps, LN_C[2, 0], 0)
                        if last and u == UNITS - 3:
                            rows(steps, ln0, LN_C[2, 0], 0)
                        if last and u == UNITS:
                            row_low(ln0, LN_C[2, 0], 0)
                            row_stats(steps, LN_C[2, 1], 1)
                        if last and u == UNITS + 1:
                            rows(steps, ln0, LN_C[2, 1], 1)

                step(0, range(1))
                row_stats(steps, LN_FIRST + 1, LN_FIRST + 1, 16 * (hf + 1))
                rows(steps, ln0, LN_FIRST + 1, LN_FIRST + 1)
                step(0, range(1, LAG - 1))
                row_low(ln0, LN_FIRST + 1, LN_FIRST + 1)
                step(0, range(LAG - 1, LAG))
                with dve.Fori(0, HKV - 1) as g:
                    step(g, range(LAG, UNITS + LAG))
                step(HKV - 1, range(LAG, UNITS + LAG), last=True)

                wide_c = wide0 + HKV * HB * BURST

                def add_layer(t):
                    dve.wait_ge(biased, hf * HT + t + 1)
                    for n in range(NN):
                        dve.wait_ge(wide_mm, wide_c + t * NN + n + 1)
                        part = acc[:, t, n * BANK:(n + 1) * BANK]
                        dve.tensor_tensor(part, part, out_ps[t % 2 * NN + n][:, :], ALU.add).then_inc(wide_free, 1)
                    dve.wait_ge(wide_free, BURST + wide_c - A_WIDE + (t + 1) * NN)
                    dve.sem_inc(out_ready, 1)

                for t in range(HT):
                    o = t - LN_LAG
                    if t >= 1:
                        add_layer(t - 1)
                    if o >= 1:
                        row_low(ln0, LN_C[1, o - 1], o - 1)
                    if o >= 0:
                        row_stats(steps, LN_C[1, o], o, 16 * (hf + 2))
                        rows(steps, ln0, LN_C[1, o], o)
                    if t + 1 < HT:
                        row_low(ln0, LN_C[2, t + 1], t + 1)
                    if t + 2 < HT:
                        row_stats(steps, LN_C[2, t + 2], t + 2)
                        rows(steps, ln0, LN_C[2, t + 2], t + 2)
                add_layer(HT - 1)
                row_low(ln0, LN_C[1, LN_FIRST - 1], LN_FIRST - 1)
                assert steps.n == LN_HALF * LN_STEPS

        @block.gpsimd
        def _(pool):
            pool.sem_inc(rope_cosd, 2)
            for s in range(2):
                pool.sem_inc(k_stored[s], 16)
            pool.sem_inc(v_stored, 16)
            pool.memset(ident[:, :], 0.0).then_inc(ident_step, 1)
            pool.wait_ge(ident_step, 1)
            pool.affine_select(out=ident[:, :], in_=ident[:, :], compare_op=ALU.not_equal, fill=1.0, base=0,
                               pattern=[[-1, P]], channel_multiplier=1).then_inc(ident_ok, 1)

            def rope_first(n, slot=0, slots=1):
                pool.wait_ge(rope_lo, 2 + n - slots + 1)
                pool.wait_ge(rope_in, 2 + n + 1)
                pool.tensor_tensor(ropes[slot][1], ropes[slot][0], cos_t[:, :], ALU.mult).then_inc(rope_cosd, 1)

            def split_lo(k, slot, parts_hi, parts_lo):
                pool.wait_ge(w_hi, k + 1)
                src = raw[:, slot, :]
                if len(parts_hi.shape) == 3:
                    src = src.rearrange("p (c n) -> p c n", c=C)
                pool.tensor_tensor(parts_lo, src, parts_hi.bitcast(F32), ALU.subtract).then_inc(w_lo, 1)

            for k in range(C, C + POOL_PIECES):
                parts = wv_s[:, k % C]
                pool.wait_ge(w_hi, k + 1)
                pool.tensor_tensor(parts[:, LO, :], a_raw[k % A_SLOTS], parts[:, HI, :].bitcast(F32),
                                   ALU.subtract).then_inc(wv_lo, 1)
            pool.wait_ge(tables_in, 32)

            def batch(b):
                def add_term(i):
                    pool.wait_ge(term_ready, b * POOL_LEVELS + i + 1)
                    if i == 0:
                        pool.sem_inc(term_used, 1)
                    else:
                        pool.wait_ge(term_used, b * POOL_LEVELS + i)
                        pool.tensor_tensor(sum_p, sum_p, term_p[i % 2], ALU.add).then_inc(term_used, 1)

                beside = ((0,), (1,), (2,), (), (3,), (4,), (), (5,))
                for g in range(HKV):
                    rope_first(b * HKV + g, g % 2, 2)
                    for i in beside[g]:
                        add_term(i)
                for i in range(6, POOL_LEVELS):
                    add_term(i)

            with pool.Fori(0, NB - 1) as b:
                batch(b)
            batch(NB - 1)
            for h in range(REP):
                split_lo(A_PIECES + h, h % 2, wq_s[:, h, :, HI, :], wq_s[:, h, :, LO, :])

            with pool.Fori(0, NH) as hf:
                piece = A_PIECES + hf * HALF_PIECES
                r_half = A_ROPES + hf * HALF_UNITS
                rope_first(r_half)
                rope_first(r_half + 1)

                def step(g, units, last=False):
                    n0 = hf * HALF_UNITS + g * UNITS
                    r0 = r_half + g * UNITS
                    p0 = piece + REP + g * 2 * REP
                    for u in units:
                        if not last or u < UNITS:
                            pool.wait_ge(inv_ready, n0 + u + 1)
                            hold(pool)
                            for t in range(TS):
                                done = pool.tensor_scalar(probs[:, u % 2, t, :], probs[:, u % 2, t, :],
                                                          row_inv[:, u % 2, t:t + 1], 1.0, ALU.mult, ALU.mult)
                            done.then_inc(p_ready, 1)
                        if not last or u + AHEAD < UNITS:
                            rope_first(r0 + u + AHEAD)
                        h = (u - WO_SPLIT) % UNITS
                        if h < REP and (not last or u < UNITS):
                            split_lo(p0 + (u - WO_SPLIT) // UNITS * 2 * REP + h, h % 2,
                                     wo_s[:, h, HI, :], wo_s[:, h, LO, :])
                        h = u - WQ_SPLIT
                        if h in range(REP) and not last:
                            split_lo(p0 + REP + h, h % 2, wq_s[:, h, :, HI, :], wq_s[:, h, :, LO, :])

                step(0, range(LAG))
                with pool.Fori(0, HKV - 1) as g:
                    step(g, range(LAG, UNITS + LAG))
                step(HKV - 1, range(LAG, UNITS + LAG), last=True)

                pool.wait_ge(bias_in, 16 * (hf + 1))
                for t in range(HT):
                    pool.wait_ge(ln_rows, hf * LN_HALF + LN_C[2, t] + 1)
                    pool.tensor_tensor(acc[:, t, :], acc[:, t, :], bias_t, ALU.add).then_inc(biased, 1)
                for h in range(REP):
                    split_lo(piece + HALF_PIECES + h, h % 2, wq_s[:, h, :, HI, :], wq_s[:, h, :, LO, :])


_INS = ("x", "ctx_4096", "mask_BxSxS2_ff0", "L0_xattn_wq", "L0_xattn_wk", "L0_xattn_wv", "L0_xattn_wo",
        "L0_ffn_qweight", "L0_ffn_lut4", "L0_ffn_bias")


def _rope_tables(positions, width):
    import numpy as np

    f = np.float32
    inv = f(1.0) / np.power(f(10000.0), np.arange(0, width, 2, dtype=f) / f(width))
    angle = (np.arange(positions, dtype=f)[None, :] * inv.astype(f)[:, None]).astype(f)
    cos, sin = np.cos(angle).astype(f), np.sin(angle).astype(f)
    return np.concatenate([cos, cos]), np.concatenate([sin, -sin])


def kernel(**inputs):
    import numpy as np
    import concourse.bacc as bacc
    from concourse import mybir
    from concourse.bass_utils import run_bass_kernel_spmd

    nc = bacc.Bacc("TRN2", target_bir_lowering=False, num_devices=1)
    arrays = {name: np.ascontiguousarray(inputs[name]) for name in _INS}
    shape = arrays["x"].shape
    arrays["rope_cos"], arrays["rope_sin"] = _rope_tables(shape[1], 128)
    args = [nc.dram_tensor(f"in_{n}", a.shape, mybir.dt.from_np(a.dtype), kind="ExternalInput").ap()
            for n, a in arrays.items()]
    out = nc.dram_tensor("out_y", shape, mybir.dt.float32, kind="ExternalOutput").ap()
    build_xattn_ffn(nc, *args, out)
    r = run_bass_kernel_spmd(nc, [{f"in_{n}": a for n, a in arrays.items()}], core_ids=[0])
    return r.results[0]["out_y"]
```

```python
class Steps:

    def __init__(self, eng, sem, base):
        self.eng, self.sem, self.base, self.n = eng, sem, base, 0

    def mark(self, instruction):
        instruction.then_inc(self.sem, 1)
        self.n += 1

    def wait(self):
        self.eng.wait_ge(self.sem, self.base + self.n)


def build_xattn_ffn(nc, x, ctx, mask, wq, wk, wv, wo, qweight, lut4, bias, rope_cos, rope_sin, out):
    from contextlib import ExitStack

    from concourse import mybir

    F32, F32R, I32 = mybir.dt.float32, mybir.dt.float32r, mybir.dt.int32
    ALU, ACT = mybir.AluOpType, mybir.ActivationFunctionType

    P = 128
    NB, S, D = x.shape
    DK = P
    HQ, HKV = wq.shape[1] // DK, wk.shape[1] // DK
    REP = HQ // HKV
    C = D // P
    TS = S // P
    NH = 2
    HB = NB // NH
    HT = HB * TS
    UNITS = HB * REP
    BITS = 4
    LEVELS = 1 << BITS
    BANK = 512
    NN = D // BANK
    EPS = 1e-5
    SCALE = float(DK) ** -0.5
    HI, LO = 0, 1
    PASSES = ((HI, HI), (HI, LO), (LO, HI))
    assert (S, DK, TS, NN, REP, HB, C) == (256, 128, 2, 2, 4, 4, 8)

    A_ROPES = NB * HKV
    HALF_UNITS = HKV * UNITS
    A_WIDE = 1 + NB * TS * NN
    BURST = TS * NN
    HALF_WIDE = HKV * HB * BURST + HT * NN
    A_PIECES = 2 * C
    POOL_PIECES = C // 2
    A_LOW = A_PIECES - POOL_PIECES
    HALF_PIECES = HKV * 2 * REP
    A_SLOTS = 7
    A_TURNS = 3
    V0, V1, V2, D0, D1, V3 = range(6)
    STAGED = 6
    K_TURNS = {V1: 4, D0: 5, V3: 6}
    V_TURNS = {V0: 0, V2: 1, D1: 2}
    POOL_LEVELS = 11
    CODE_STEPS = 1 + (BITS - 1) + 1
    AHEAD, LAG = 2, 3
    WO_SPLIT, WQ_SPLIT = 1, UNITS - REP - 1
    DQ_STEPS = CODE_STEPS + 1 + 2 * (LEVELS - POOL_LEVELS - 1)
    LN_LAG = 2
    SIDE = ({4: 5, 6: 6, 8: 7}, {6: 6, 8: 7})
    LN_ORDER = [(0, 1, t) for t in range(HT)]
    for hf in range(NH):
        for t in range(HT + 1):
            if t < HT:
                LN_ORDER.append((hf, 2, t))
            if hf + 1 < NH and t - 1 >= LN_LAG:
                LN_ORDER.append((hf + 1, 1, t - 1 - LN_LAG))
        if hf + 1 < NH:
            LN_ORDER += [(hf + 1, 1, t) for t in SIDE[hf + 1].values()]
    LN = {key: e for e, key in enumerate(LN_ORDER)}
    LN_SIDE = [(hf, 1, t) for hf in range(NH) for t in SIDE[hf].values()]
    LN_BANKS = {(0, 1, 0): (0, 1), (0, 1, 1): (2, 5), (0, 1, 2): (6, 7), (0, 1, 3): (1, 4), (0, 1, 4): (6, 7)}
    for key in LN_ORDER:
        if key not in LN_SIDE and key not in LN_BANKS:
            LN_BANKS[key] = ((2, 5), (0, 3))[len(LN_BANKS) % 2]
    LN_SPLIT = {key: n + 1 for n, key in enumerate(LN_BANKS)}
    LN_FREE = {key: max([0] + [n for other, n in LN_SPLIT.items() if n < LN_SPLIT[key]
                               and set(LN_BANKS[other]) & set(LN_BANKS[key])]) for key in LN_BANKS}

    x_tiles = x.rearrange("b (t p) d -> (b t) p d", p=P)
    out_tiles = out.rearrange("b (t p) d -> (b t) p d", p=P)
    ctx_tiles = ctx.rearrange("b (t p) d -> b t p d", p=P)
    mask_v = mask.rearrange("b (t p) k -> b p t k", p=P)
    wk_v = wk.rearrange("(c p) n -> c p n", p=P)
    wv_v = wv.rearrange("(c p) n -> c p n", p=P)
    wq_v = wq.rearrange("(c p) (h n) -> h p c n", p=P, n=DK)
    wo_v = wo.rearrange("(h p) n -> h p n", p=DK)
    qw_v = qweight[0:BITS].rearrange("k (t p) w -> t p k w", p=P)
    lut_v = lut4.rearrange("(t p) l -> t p l", p=P)
    bias_v = bias.rearrange("(a n) -> a n", a=1)
    k_scr = nc.dram_tensor("k_scratch", (HKV, NB, P, 2 * S), F32, kind="Internal").ap()
    v_scr = nc.dram_tensor("v_scratch", (NB, TS, 2, P, HKV * DK), F32, kind="Internal").ap()
    w_scr = nc.dram_tensor("w_scratch", (P, 2, C, D), F32, kind="Internal").ap()

    with ExitStack() as stack:
        def sb(name, shape, dt):
            return stack.enter_context(nc.sbuf_tensor(name, shape, dt))

        def sem(name):
            return stack.enter_context(nc.semaphore(name))

        W = sb("weights_split", [P, 2 * C * D], F32R)
        X = sb("acts_split", [P, 2 * C * D], F32R)
        R = sb("small_split", [P, 6144], F32R)
        wk_s = W[:, :].rearrange("p (c l n) -> p c l n", c=C, l=2)
        wv_s = X[:, :].rearrange("p (c l n) -> p c l n", c=C, l=2)
        ctxT = R[:, 0:4096].rearrange("p (c l n) -> p c l n", c=C, l=2)
        k_stage = R[:, 4096:5120].rearrange("p (s l n) -> p s l n", s=2, l=2)
        k_stage_all, v_stage_all = R[:, 4096:5120], R[:, 5120:6144]
        wq_s = W[:, 0:8192].rearrange("p (h c l n) -> p h c l n", h=REP, c=C, l=2)
        wo_s = W[:, 8192:16384].rearrange("p (h l n) -> p h l n", h=REP, l=2)
        xT = X[:, :].rearrange("p (c l n) -> p c l n", c=C, l=2)
        q_s = R[:, 0:2048].rearrange("p (s l n) -> p s l n", s=4, l=2)
        o_s = R[:, 2048:3072].rearrange("p (s l n) -> p s l n", s=2, l=2)
        k_s = R[:, 3072:3584].rearrange("p (l n) -> p l n", l=2)
        v_s = R[:, 4608:5120].rearrange("p (k l n) -> p k l n", k=TS, l=2)
        pT_s = R[:, 5120:6144].rearrange("p (l k n) -> p l k n", l=2, k=TS)
        w4_s = W[:, :].rearrange("p (c l n) -> p c l n", c=C, l=2)

        acc_t = sb("residual", [P, HT * D], F32)
        acc = acc_t[:, :].rearrange("p (t n) -> p t n", t=HT)
        ctx_stage = acc_t[:, 0:2048].rearrange("p (t n) -> p t n", t=TS)
        codes = acc_t[:, 2048:3072].bitcast(I32)
        term_v = acc_t[:, 3072:4096]
        sum_v = acc_t[:, 4096:5120]
        sum_p = acc_t[:, 6144:7168]
        planes = acc_t[:, 7168:7296].bitcast(I32).rearrange("p (k w) -> p k w", k=BITS)
        spread = acc_t[:, 7296:7808].bitcast(I32).rearrange("p (r k w) -> p r k w", r=4, k=BITS)
        nibbles = acc_t[:, 7808:7936].bitcast(I32).rearrange("p (r w) -> p r w", r=4)
        lut_t = acc_t[:, 7936:7936 + LEVELS]
        raw_t = sb("raw", [P, 2 * D], F32)
        raw = raw_t[:, :].rearrange("p (s n) -> p s n", s=2)
        a_raw = [raw[:, 0, :], raw[:, 1, :]] + [acc_t[:, i * D:(i + 1) * D] for i in range(2, A_SLOTS)]
        ln_row = sb("ln_row", [P, D], F32)
        term_p = [acc_t[:, 5120:6144], ln_row[:, :]]
        prob_t = sb("probs", [P, 2 * TS * S], F32)
        probs = prob_t[:, :].rearrange("p (s t k) -> p s t k", s=2, t=TS)
        bias_t = prob_t[:, :]
        mask_t = sb("mask_tile", [P, TS, S], F32)
        rope_x = sb("rope_x", [P, S], F32)
        rope_a = sb("rope_a", [P, S], F32)
        rope_b = sb("rope_b", [P, S], F32)
        ropes = [(rope_x[:, :], rope_a[:, :], rope_b[:, :]), tuple(prob_t[:, i * S:(i + 1) * S] for i in range(3))]
        cos_t = sb("cos_t", [P, S], F32)
        sin_t = sb("sin_t", [P, S], F32)
        ident = sb("ident", [P, P], F32)
        stat_t = sb("row_numbers", [P, 56], F32)
        neg_max, row_max, row_sum, row_inv = (
            stat_t[:, i * 2 * TS:(i + 1) * 2 * TS].rearrange("p (s t) -> p s t", s=2) for i in range(4))
        ln_stat = stat_t[:, 16:40].rearrange("p (s n k) -> p s n k", s=2, n=2)
        ln_mv = stat_t[:, 40:44].rearrange("p (s k) -> p s k", s=2)
        ln_ve, ln_sd, ln_y, ln_e, ln_f, ln_r = (stat_t[:, 44 + 2 * i:46 + 2 * i] for i in range(6))

        bank = [stack.enter_context(nc.psum_tensor(f"bank{i}", [P, BANK], F32)) for i in range(8)]
        ctx_ps = [bank[i] for i in (0, 1, 2, 5)]
        w4_ps = [bank[3], bank[4]]
        k_ps = [bank[3][:, 0:S], bank[4][:, 0:S]]
        q_ps = bank[3][:, 0:S]
        wide_ps = [bank[6], bank[7]]
        out_ps = [bank[1], bank[4], bank[6], bank[7]]
        s_ps = bank[0]
        pT_ps = bank[2]
        o_ps = bank[5][:, 0:S]
        ln_ps = {key: [bank[i] for i in banks] for key, banks in LN_BANKS.items()}

        tables_in = sem("tables_in")
        ctx_in = [sem(f"ctx_in{t}") for t in range(TS)]
        planes_in, lut_in = sem("planes_in"), sem("lut_in")
        a_raw_in = [sem(f"raw_in{s}") for s in range(A_SLOTS)]
        raw_in = a_raw_in[0:2]
        x_in = [sem(f"x_in{t}") for t in range(HT)]
        k_in, v_in, mask_in = sem("k_in"), sem("v_in"), sem("mask_in")
        w4_in = [sem(f"w4_in{c}") for c in range(C)]
        bias_in = sem("bias_in")
        k_stored = [sem(f"k_stored{s}") for s in range(2)]
        v_stored = sem("v_stored")
        out_stored = sem("out_stored")
        ident_step, ident_ok = sem("ident_step"), sem("ident_ok")
        w_hi, w_lo, wv_lo = sem("w_hi"), sem("w_lo"), sem("wv_lo")
        ctx_tr, ctx_hi, ctx_lo = sem("ctx_tr"), sem("ctx_hi"), sem("ctx_lo")
        ctx_used = sem("ctx_used")
        stage_hi, stage_lo = sem("stage_hi"), sem("stage_lo")
        dq_step = sem("dq_step")
        term_ready, term_used = sem("term_ready"), sem("term_used")
        w4_ready, w4_tr = sem("w4_ready"), sem("w4_tr")
        rope_mm, rope_in = sem("rope_mm"), sem("rope_in")
        rope_cosd, rope_sind = sem("rope_cosd"), sem("rope_sind")
        rope_sum, rope_hi, rope_lo = sem("rope_sum"), sem("rope_hi"), sem("rope_lo")
        wide_mm, wide_free = sem("wide_mm"), sem("wide_free")
        s_mm, s_read, s_max = sem("s_mm"), sem("s_read"), sem("s_max")
        exp_done, inv_ready = sem("exp_done"), sem("inv_ready")
        p_ready, pT_tr, pT_hi, pT_lo = sem("p_ready"), sem("pT_tr"), sem("pT_hi"), sem("pT_lo")
        o_mm, o_hi, o_lo = sem("o_mm"), sem("o_hi"), sem("o_lo")
        ln_step, ln_var, ln_std = sem("ln_step"), sem("ln_var"), sem("ln_std")
        side_tr, side_hi, side_lo = sem("side_tr"), sem("side_hi"), sem("side_lo")
        ln_rows, ln_tr, ln_hi, ln_lo = sem("ln_rows"), sem("ln_tr"), sem("ln_hi"), sem("ln_lo")
        biased, out_ready, w4_used = sem("biased"), sem("out_ready"), sem("w4_used")
        held = sem("held")

        def beside(hf, u):
            for j in range(2):
                if u - j in SIDE[hf]:
                    return (hf, 1, SIDE[hf][u - j]), j

        def staging(i):
            return (k_stage_all, k_stored[0]) if i in K_TURNS else (v_stage_all, v_stored)

        def hold(eng):
            eng.sem_inc(held, 1)

        block = stack.enter_context(nc.Block())

        @block.sync
        def _(sp):
            def load_piece(src, stage, arrived):
                if len(src.shape) == 3:
                    stage = stage.rearrange("p (c n) -> p c n", c=C)
                sp.dma_start(stage, src).then_inc(arrived, 16)

            def load_raw(k, src, slot):
                sp.wait_ge(w_lo, A_LOW + k - 1)
                load_piece(src, raw[:, slot, :], raw_in[slot])

            for t in range(TS):
                sp.dma_start(ctx_stage[:, t, :], ctx_tiles[0, t]).then_inc(ctx_in[t], 16)
            for k in range(A_PIECES):
                if A_SLOTS <= k < A_SLOTS + C:
                    sp.wait_ge(w_lo, k - A_SLOTS + 1)
                elif k >= A_SLOTS + C:
                    sp.wait_ge(wv_lo, k - A_SLOTS - C + 1)
                load_piece((wk_v, wv_v)[k // C][k % C], a_raw[k % A_SLOTS], a_raw_in[k % A_SLOTS])
                if k == C - 1:
                    sp.dma_start(cos_t[:, :], rope_cos).then_inc(tables_in, 16)
                    sp.dma_start(sin_t[:, :], rope_sin).then_inc(tables_in, 16)
                    sp.dma_start(planes, qw_v[0]).then_inc(planes_in, 16)
                    sp.dma_start(lut_t, lut_v[0]).then_inc(lut_in, 16)

            def load_keys(hf, g, b):
                n = hf * HALF_UNITS + g * UNITS + b * REP
                sp.wait_ge(s_mm, n + 1)
                hold(sp)
                sp.dma_start(k_s.bitcast(F32).rearrange("p l n -> p (l n)"), k_scr[g, hf * HB + b]).then_inc(k_in, 16)
                sp.wait_ge(s_read, n + 1)
                hold(sp)
                sp.dma_start(mask_t[:, :, :], mask_v[hf * HB + b]).then_inc(mask_in, 16)

            def batch(b, last=False):
                if last:
                    sp.wait_ge(ctx_tr, 4 * NB)
                    for t in range(TS):
                        sp.dma_start(acc[:, t, :], x_tiles[t]).then_inc(x_in[t], 16)
                    for h in range(2):
                        load_raw(h, wq_v[h], h)
                else:
                    sp.wait_ge(ctx_tr, 4 * b + 4)
                    hold(sp)
                    for t in range(TS):
                        sp.dma_start(ctx_stage[:, t, :], ctx_tiles[b + 1, t]).then_inc(ctx_in[t], 16)
                for g in range(HKV):
                    sp.wait_ge(rope_lo, 2 + b * HKV + g + 1)
                    sp.dma_start(k_scr[g, b], k_stage[:, g % 2].bitcast(F32)
                                 .rearrange("p l n -> p (l n)")).then_inc(k_stored[g % 2], 16)
                if not last:
                    sp.dma_start(planes, qw_v[b + 1]).then_inc(planes_in, 16)

                def store_values(i, t, n):
                    sp.wait_ge(stage_lo, STAGED // 2 + b * STAGED + i + 1)
                    stage, stored = staging(i)
                    sp.dma_start(v_scr[b, t, :, :, n * BANK:(n + 1) * BANK].rearrange("l p n -> p l n"),
                                 stage.bitcast(F32).rearrange("p (l n) -> p l n", l=2)).then_inc(stored, 16)

                def store_weights(i, j):
                    sp.wait_ge(stage_lo, STAGED // 2 + b * STAGED + i + 1)
                    stage, stored = staging(i)
                    dst = w_scr.rearrange("p j k (t n) -> t j p k n", n=P)
                    sp.dma_start(dst[b, j], stage.bitcast(F32).rearrange("p (k n) -> p k n", n=P)
                                 ).then_inc(stored, 16)

                def load_rows(tiles):
                    for t in tiles:
                        sp.dma_start(acc[:, t, :], x_tiles[t]).then_inc(x_in[t], 16)

                store_values(V0, 0, 0)
                store_values(V1, 0, 1)
                store_values(V2, 1, 0)
                store_weights(D0, 0)
                if not last:
                    sp.dma_start(lut_t, lut_v[b + 1]).then_inc(lut_in, 16)
                else:
                    sp.wait_ge(w4_tr, 2 * NB)
                    load_rows((2, 3))
                    load_raw(2, wq_v[2], 0)
                store_weights(D1, 1)
                if last:
                    sp.wait_ge(k_stored[0], 16 * NB * (HKV // 2 + len(K_TURNS)))
                    sp.wait_ge(k_stored[1], 16 + 16 * NB * (HKV // 2))
                    sp.wait_ge(wide_mm, A_WIDE)
                    load_keys(0, 0, 0)
                    load_rows((4,))
                    load_raw(3, wq_v[3], 1)
                store_values(V3, 1, 1)
                if last:
                    load_rows(range(5, HT))

            with sp.Fori(0, NB - 1) as b:
                batch(b)
            batch(NB - 1, last=True)
            sp.wait_ge(k_stored[0], 16 + 16 * NB * (HKV // 2 + len(K_TURNS)))
            sp.wait_ge(k_stored[1], 16 + 16 * NB * (HKV // 2))
            sp.wait_ge(v_stored, 16 + 16 * NB * len(V_TURNS))

            def half(hf):
                piece = hf * HALF_PIECES

                def load_step(g, first=False, last=False):
                    n0 = hf * HALF_UNITS + g * UNITS
                    for b in range(HB):
                        batch = hf * HB + b
                        n = n0 + b * REP

                        def load_values():
                            sp.wait_ge(o_mm, n + 1)
                            hold(sp)
                            v_src = v_scr[batch].rearrange("k l p (g n) -> g p (k l) n", n=DK)
                            sp.dma_start(v_s.bitcast(F32).rearrange("p k l n -> p (k l) n"),
                                         v_src[g]).then_inc(v_in, 16)

                        if not (first and b == 0):
                            load_keys(hf, g, b)
                        if b == 0:
                            for h in range(REP - 1):
                                if h == 2:
                                    load_values()
                                load_raw(piece + REP + g * 2 * REP + h, wo_v[g * REP + h], h % 2)
                        if b == 1:
                            load_raw(piece + REP + g * 2 * REP + REP - 1, wo_v[g * REP + REP - 1], (REP - 1) % 2)
                        if b in (1, 2):
                            load_values()
                        if b >= 2 and not last:
                            for h in (2 * b - 4, 2 * b - 3):
                                load_raw(piece + 2 * REP + g * 2 * REP + h, wq_v[(g + 1) * REP + h], h % 2)
                        if b == HB - 1:
                            load_values()

                load_step(0, first=True)
                with sp.Fori(1, HKV - 1) as g:
                    load_step(g)
                load_step(HKV - 1, last=True)
                units = (hf + 1) * HALF_UNITS
                for c in range(C):
                    if c == 0:
                        sp.wait_ge(rope_mm, A_ROPES + units)
                    elif c == REP:
                        sp.wait_ge(o_mm, 1 + units - 1)
                    elif c == REP + 1:
                        sp.wait_ge(o_mm, 1 + units)
                    elif c == REP + 2:
                        sp.wait_ge(wide_mm, A_WIDE + hf * HALF_WIDE + HKV * HB * BURST)
                    hold(sp)
                    w4_src = w_scr.rearrange("p j (l c) n -> j c p l n", l=2)
                    sp.dma_start(w4_s[:, c].bitcast(F32), w4_src[c // 4, c % 4]).then_inc(w4_in[c], 16)
                    if c == REP + 1:
                        sp.wait_ge(pT_tr, 2 + units)
                        sp.dma_start(bias_t, bias_v.to_broadcast([P, D])).then_inc(bias_in, 16)
                if hf + 1 < NH:
                    load_keys(hf + 1, 0, 0)
                    for h in range(2):
                        load_raw(piece + HALF_PIECES + h, wq_v[h], h)
                for t in range(HT):
                    sp.wait_ge(out_ready, hf * HT + t + 1)
                    sp.dma_start(out_tiles[hf * HT + t], acc[:, t, :]).then_inc(out_stored, 16)
                    if hf + 1 < NH:
                        sp.wait_ge(out_stored, 16 * (hf * HT + t + 1))
                        sp.dma_start(acc[:, t, :], x_tiles[(hf + 1) * HT + t]).then_inc(x_in[t], 16)
                        if t == HT - 2:
                            for h in range(2, REP):
                                load_raw(piece + HALF_PIECES + h, wq_v[h], h % 2)

            for hf in range(NH):
                half(hf)
            sp.wait_ge(out_stored, 16 * NH * HT)

        @block.tensor
        def _(pe):
            pe.sem_inc(s_mm, 1)
            pe.sem_inc(o_mm, 1)
            pe.sem_inc(pT_tr, 2)
            pe.sem_inc(wide_mm, 1)
            pe.wait_ge(ident_ok, 1)

            def turn_context(loaded):
                for t in range(TS):
                    pe.wait_ge(ctx_in[t], loaded)
                    for c in range(C):
                        col = (c % 2) * S + t * P
                        last = pe.transpose(ctx_ps[c // 2][:, col:col + P],
                                            ctx_stage[:, t, c * P:(c + 1) * P], ident[:, :])
                        if t == TS - 1 and c % 2:
                            last.then_inc(ctx_tr, 1)

            turn_context(16)

            def turn_rows(key):
                pe.wait_ge(ln_rows, LN[key] + 1)
                if LN_FREE[key]:
                    pe.wait_ge(ln_lo, LN_FREE[key])
                for c in range(C):
                    last = pe.transpose(ln_ps[key][c // 4][:, (c % 4) * P:(c % 4 + 1) * P],
                                        ln_row[:, c * P:(c + 1) * P], ident[:, :])
                last.then_inc(ln_tr, 1)

            def batch(b, last=False):
                for g in range(HKV):
                    if g < 2:
                        pe.wait_ge(stage_lo, b * STAGED + g + 1)
                    pe.wait_ge(rope_in, b * HKV + g + 1)
                    for c in range(C):
                        if g == 0:
                            pe.wait_ge(w_lo, c + 1)
                            pe.wait_ge(ctx_lo, 4 * b + c // 2 + 1)
                        for i, (a, m) in enumerate(PASSES):
                            done = pe.matmul(k_ps[g % 2], wk_s[:, c, a, g * DK:(g + 1) * DK],
                                             ctxT[:, c, m, :], start=c == 0 and i == 0,
                                             stop=c == C - 1 and i == 2)
                    done.then_inc(rope_mm, 1)

                def turn_weights():
                    pe.wait_ge(rope_in, 2 + (b + 1) * HKV)
                    pe.wait_ge(w4_ready, b + 1)
                    for c in range(C):
                        done = pe.transpose(w4_ps[c // 4][:, (c % 4) * P:(c % 4 + 1) * P],
                                            sum_v[:, c * P:(c + 1) * P], ident[:, :])
                        if c % 4 == 3:
                            done.then_inc(w4_tr, 1)

                def values(t, n, split):
                    pe.wait_ge(stage_lo, split)
                    for c in range(C):
                        for i, (a, m) in enumerate(PASSES):
                            done = pe.matmul(wide_ps[n][:, :], ctxT[:, c, a, t * P:(t + 1) * P],
                                             wv_s[:, c, m, n * BANK:(n + 1) * BANK],
                                             start=c == 0 and i == 0, stop=c == C - 1 and i == 2)
                        if not last and t == TS - 1 and n == NN - 1 and c in (1, 3, 5):
                            done.then_inc(ctx_used, 1)
                        if last and t == TS - 1 and n == NN - 1:
                            if c == 1:
                                turn_weights()
                                turn_rows((0, 1, 0))
                            if c == 4:
                                turn_rows((0, 1, 1))
                    done.then_inc(wide_mm, 1)

                pe.wait_ge(w_lo, A_LOW)
                pe.wait_ge(wv_lo, POOL_PIECES)
                values(0, 0, 2 + b * STAGED)
                values(0, 1, STAGED // 2 + b * STAGED)
                values(1, 0, STAGED // 2 + b * STAGED + V0 + 1)
                if not last:
                    turn_context(16 * (b + 2))
                    turn_weights()
                values(1, 1, STAGED // 2 + b * STAGED + V1 + 1)

            with pe.Fori(0, NB - 1) as b:
                batch(b)
            batch(NB - 1, last=True)

            def half(hf):
                piece = A_LOW + hf * HALF_PIECES
                wide0 = A_WIDE + hf * HALF_WIDE

                def query(r, wanted, u, first):
                    b, h = u // REP % HB, u % REP
                    if b == 0:
                        pe.wait_ge(w_lo, wanted)
                    if first and h == 0:
                        for key in ((hf, 1, b * TS + t) for t in range(TS)):
                            if key in LN_SIDE:
                                pe.wait_ge(side_lo, 2 * LN_SIDE.index(key) + 2)
                            else:
                                pe.wait_ge(ln_lo, LN_SPLIT[key])
                    pe.wait_ge(rope_in, 2 + r)
                    for c in range(C):
                        for i, (a, m) in enumerate(PASSES):
                            last = pe.matmul(q_ps, wq_s[:, h, c, a, :],
                                             xT[:, c, m, b * S:(b + 1) * S],
                                             start=c == 0 and i == 0, stop=c == C - 1 and i == 2)
                    last.then_inc(rope_mm, 1)

                r_half = A_ROPES + hf * HALF_UNITS
                if hf:
                    pe.wait_ge(ln_lo, LN_SPLIT[hf, 1, HT - LN_LAG - 2])
                query(r_half, piece + 1, 0, True)
                query(r_half + 1, piece + 2, 1, True)
                if hf == 0:
                    turn_rows((0, 1, 2))
                else:
                    pe.wait_ge(ln_lo, LN_SPLIT[hf, 1, HT - LN_LAG - 1])

                def step(g, units, first=False, last=False):
                    n0 = hf * HALF_UNITS + g * UNITS
                    w0 = wide0 + g * HB * BURST
                    r0 = r_half + g * UNITS

                    def scores(u):
                        if u % REP == 0:
                            pe.wait_ge(k_in, 16 * (hf * HKV * HB + g * HB + u // REP + 1))
                        pe.wait_ge(rope_lo, 2 + r0 + u + 1)
                        pe.wait_ge(s_read, n0 + u + 1)
                        for t in range(TS):
                            for i, (a, m) in enumerate(PASSES):
                                last = pe.matmul(s_ps[:, t * S:(t + 1) * S],
                                                 q_s[:, u % 4, a, t * P:(t + 1) * P], k_s[:, m, :],
                                                 start=i == 0, stop=i == 2)
                        last.then_inc(s_mm, 1)

                    def turn_side(key, j, u):
                        pe.wait_ge(ln_rows, LN[key] + 1)
                        pe.wait_ge(pT_lo, n0 + u)
                        for c in range(4):
                            last = pe.transpose(pT_ps[:, c * P:(c + 1) * P],
                                                ln_row[:, (4 * j + c) * P:(4 * j + c + 1) * P], ident[:, :])
                        last.then_inc(ln_tr if j else side_tr, 1)

                    def turn(u):
                        pe.wait_ge(p_ready, n0 + u + 1)
                        pe.wait_ge(pT_lo, n0 + u + 1)
                        for t in range(TS):
                            for k in range(TS):
                                last = pe.transpose(pT_ps[:, k * S + t * P:k * S + (t + 1) * P],
                                                    probs[:, u % 2, t, k * P:(k + 1) * P], ident[:, :])
                        last.then_inc(pT_tr, 1)

                    def attend(u):
                        if u % REP == 0:
                            pe.wait_ge(v_in, 16 * (hf * HKV * HB + g * HB + u // REP + 1))
                        pe.wait_ge(pT_lo, 1 + n0 + u + 1)
                        pe.wait_ge(o_lo, n0 + u + 1)
                        for k in range(TS):
                            for i, (a, m) in enumerate(PASSES):
                                last = pe.matmul(o_ps, v_s[:, k, a, :], pT_s[:, m, k, :],
                                                 start=k == 0 and i == 0, stop=k == TS - 1 and i == 2)
                        last.then_inc(o_mm, 1)

                    def project(u):
                        b, h = u // REP, u % REP
                        if b == 0:
                            pe.wait_ge(w_lo, piece + REP + g * 2 * REP + h + 1)
                        if first and hf == 0 and u == 0:
                            pe.wait_ge(ln_lo, LN_SPLIT[0, 1, 4])
                        pe.wait_ge(o_lo, 1 + n0 + u + 1)
                        for part in range(BURST):
                            t, n = part // NN, part % NN
                            if h == 0:
                                pe.wait_ge(wide_free, w0 - A_WIDE + b * BURST + part + 1)
                            for i, (a, m) in enumerate(PASSES):
                                last = pe.matmul(out_ps[part][:, :], o_s[:, u % 2, a, t * P:(t + 1) * P],
                                                 wo_s[:, h, m, n * BANK:(n + 1) * BANK],
                                                 start=h == 0 and i == 0, stop=h == REP - 1 and i == 2)
                            if h == REP - 1:
                                last.then_inc(wide_mm, 1)

                    for u in units:
                        if not last or u < UNITS:
                            scores(u)
                        side = beside(hf, u) if first else None
                        if side:
                            turn_side(*side, u)
                        if not last or u + AHEAD < UNITS:
                            v = u + AHEAD
                            query(r0 + v, piece + (g + v // UNITS) * 2 * REP + v % REP + 1, v,
                                  first and v < UNITS)
                        if u >= 2 and (not last or u - 2 < UNITS):
                            attend(u - 2)
                        if side:
                            pe.wait_ge(side_lo, 2 * LN_SIDE.index(side[0]) + side[1] + 1)
                        if u >= 1 and (not last or u - 1 < UNITS):
                            turn(u - 1)
                        if last and u == UNITS:
                            turn_rows((hf, 2, 0))
                        if u >= LAG:
                            project(u - LAG)

                step(0, range(1), first=True)
                if hf == 0:
                    turn_rows((0, 1, 3))
                step(0, range(1, 2), first=True)
                if hf == 0:
                    turn_rows((0, 1, 4))
                step(0, range(2, UNITS + LAG), first=True)
                with pe.Fori(1, HKV - 1) as g:
                    step(g, range(LAG, UNITS + LAG))
                step(HKV - 1, range(LAG, UNITS + LAG), last=True)

                wide_c = wide0 + HKV * HB * BURST
                for t in range(HT):
                    pe.wait_ge(ln_lo, LN_SPLIT[hf, 2, t])
                    for n in range(NN):
                        pe.wait_ge(wide_free, wide_c - A_WIDE + t * NN + n + 1)
                    for c in range(C):
                        if t == 0:
                            pe.wait_ge(w4_in[c], 16 * (hf + 1))
                        for n in range(NN):
                            for i, (a, m) in enumerate(PASSES):
                                last = pe.matmul(out_ps[t % 2 * NN + n][:, :], xT[:, c, a, t * P:(t + 1) * P],
                                                 w4_s[:, c, m, n * BANK:(n + 1) * BANK],
                                                 start=c == 0 and i == 0, stop=c == C - 1 and i == 2)
                            if c == C - 1:
                                last.then_inc(wide_mm, 1)
                        if hf + 1 < NH and t == HT - 1 and c < REP:
                            last.then_inc(w4_used, 1)
                        if c == C // 2 - 1 and t + 1 < HT:
                            turn_rows((hf, 2, t + 1))
                    if hf + 1 < NH and t >= LN_LAG:
                        turn_rows((hf + 1, 1, t - LN_LAG))

            for hf in range(NH):
                half(hf)

        @block.scalar
        def _(act):
            act.sem_inc(rope_in, 2)

            def split_hi(stage, arrived, count, dst):
                act.wait_ge(arrived, 16 * count)
                if len(dst.shape) == 3:
                    stage = stage.rearrange("p (c n) -> p c n", c=C)
                act.activation(dst, stage, ACT.Copy).then_inc(w_hi, 1)

            def rope_copy(n, product, scale, slot=0, slots=1):
                act.wait_ge(rope_cosd, 2 + n - slots + 1)
                act.wait_ge(rope_sind, 2 + n - slots + 1)
                act.wait_ge(rope_mm, n + 1)
                act.activation(ropes[slot][0], product, ACT.Copy, scale=scale).then_inc(rope_in, 1)

            def rope_high(n, dst, slot=0):
                act.wait_ge(rope_sum, n + 1)
                act.activation(dst, ropes[slot][1], ACT.Copy).then_inc(rope_hi, 1)

            def context_high(first, j):
                act.wait_ge(ctx_tr, first + j + 1)
                act.activation(ctxT[:, 2 * j:2 * j + 2, HI, :], ctx_ps[j][:, :].rearrange("p (c n) -> p c n", c=2),
                               ACT.Copy).then_inc(ctx_hi, 1)

            def row_std(key):
                s = LN[key] % 2
                act.wait_ge(ln_var, LN[key] + 1)
                act.activation(ln_sd[:, s:s + 1], ln_ve[:, s:s + 1], ACT.Sqrt).then_inc(ln_std, 1)

            def rows_high(key, chunks, src):
                t = key[2]
                return act.activation(xT[:, chunks:chunks + 4, HI, t * P:(t + 1) * P],
                                      src[:, :].rearrange("p (c n) -> p c n", c=4), ACT.Copy)

            def row_high(key):
                act.wait_ge(ln_tr, LN[key] + 1)
                for j in range(2):
                    last = rows_high(key, 4 * j, ln_ps[key][j])
                last.then_inc(ln_hi, 1)

            for j in range(4):
                context_high(0, j)
            for k in range(A_PIECES):
                split_hi(a_raw[k % A_SLOTS], a_raw_in[k % A_SLOTS], k // A_SLOTS + 1,
                         (wk_s, wv_s)[k // C][:, k % C, HI, :])

            def batch(b, last=False):
                rope_copy(b * HKV, k_ps[0], 1.0, 0, 2)
                for g in range(HKV):
                    if g + 1 < HKV:
                        rope_copy(b * HKV + g + 1, k_ps[(g + 1) % 2], 1.0, (g + 1) % 2, 2)
                    stored = b * (HKV // 2 + (0 if g % 2 else len(K_TURNS))) + g // 2 + 1
                    act.wait_ge(k_stored[g % 2], 16 * stored)
                    rope_high(b * HKV + g, k_stage[:, g % 2, HI, :], g % 2)

                def staged_high(i, src):
                    if i in K_TURNS:
                        act.wait_ge(k_stored[0], 16 * (b * (HKV // 2 + len(K_TURNS)) + K_TURNS[i] + 1))
                    else:
                        act.wait_ge(v_stored, 16 * (b * len(V_TURNS) + V_TURNS[i] + 1))
                    act.activation(staging(i)[0][:, 0:BANK], src[:, :], ACT.Copy).then_inc(stage_hi, 1)

                def values_high(i, part):
                    act.wait_ge(wide_mm, 1 + b * TS * NN + part + 1)
                    staged_high(i, wide_ps[part % 2])

                def weights_high(i, j):
                    act.wait_ge(w4_tr, b * 2 + j + 1)
                    staged_high(i, w4_ps[j])

                def next_context_high(j):
                    if j < 3:
                        act.wait_ge(ctx_used, 3 * b + j + 1)
                    else:
                        act.wait_ge(wide_mm, 1 + (b + 1) * TS * NN)
                    context_high(4 * (b + 1), j)

                values_high(V0, 0)
                act.wait_ge(k_stored[1], 16 * (b * (HKV // 2) + HKV // 2 + 1))
                values_high(V1, 1)
                if last:
                    for h in range(2):
                        split_hi(raw[:, h, :], raw_in[h], A_TURNS + 1, wq_s[:, h, :, HI, :])
                    row_std((0, 1, 0))
                    row_std((0, 1, 1))
                values_high(V2, 2)
                weights_high(D0, 0)
                if not last:
                    next_context_high(0)
                else:
                    act.wait_ge(wide_mm, A_WIDE - 1)
                    row_high((0, 1, 0))
                    row_high((0, 1, 1))
                weights_high(D1, 1)
                if not last:
                    for j in range(1, 4):
                        next_context_high(j)
                values_high(V3, 3)

            with act.Fori(0, NB - 1) as b:
                batch(b)
            batch(NB - 1, last=True)

            def half(hf):
                seen = A_TURNS + hf * (HALF_PIECES // 2)
                r_half = A_ROPES + hf * HALF_UNITS

                def first_weights(before, h):
                    split_hi(raw[:, h % 2, :], raw_in[h % 2], before + h // 2 + 1, wq_s[:, h, :, HI, :])

                if hf == 0:
                    row_std((0, 1, 2))
                rope_copy(r_half, q_ps, SCALE)
                if hf == 0:
                    row_std((0, 1, 3))
                first_weights(seen, 2)
                rope_high(r_half, q_s[:, 0, HI, :])
                if hf:
                    first_weights(seen, 3)
                rope_copy(r_half + 1, q_ps, SCALE)
                rope_high(r_half + 1, q_s[:, 1, HI, :])
                if not hf:
                    first_weights(seen, 3)
                if hf == 0:
                    row_std((0, 1, 4))
                    row_high((0, 1, 2))

                def step(g, units, first=False, last=False):
                    n0 = hf * HALF_UNITS + g * UNITS
                    r0 = r_half + g * UNITS
                    p0 = seen + REP // 2 + g * REP

                    def exponent(u):
                        act.wait_ge(s_max, n0 + u + 1)
                        for t in range(TS):
                            last = act.activation(probs[:, u % 2, t, :], probs[:, u % 2, t, :], ACT.Exp,
                                                  bias=neg_max[:, u % 2, t:t + 1],
                                                  accum_out=row_sum[:, u % 2, t:t + 1])
                        last.then_inc(exp_done, 1)

                    def turned_high(u):
                        act.wait_ge(o_mm, n0 + u + 1)
                        act.wait_ge(pT_tr, 2 + n0 + u + 1)
                        act.activation(pT_s[:, HI, :, :], pT_ps[:, :].rearrange("p (k n) -> p k n", k=TS),
                                       ACT.Copy).then_inc(pT_hi, 1)

                    def output_high(u):
                        act.wait_ge(o_mm, 1 + n0 + u + 1)
                        act.activation(o_s[:, u % 2, HI, :], o_ps, ACT.Copy).then_inc(o_hi, 1)

                    def side_high(key, j):
                        if j:
                            act.wait_ge(ln_tr, LN[key] + 1)
                        else:
                            act.wait_ge(side_tr, LN_SIDE.index(key) + 1)
                        rows_high(key, 4 * j, pT_ps).then_inc(side_hi, 1)

                    for u in units:
                        short = last and u + AHEAD >= UNITS
                        if first and beside(hf, u):
                            side_high(*beside(hf, u))
                        if not short:
                            exponent(u)
                            rope_copy(r0 + u + AHEAD, q_ps, SCALE)
                        if u >= 2 and (not last or u - 2 < UNITS):
                            output_high(u - 2)
                        if u >= 1 and (not last or u - 1 < UNITS):
                            turned_high(u - 1)
                        if short and u < UNITS:
                            exponent(u)
                        if not last or u + AHEAD < UNITS:
                            rope_high(r0 + u + AHEAD, q_s[:, (u + AHEAD) % 4, HI, :])
                        if first and u + 2 in SIDE[hf]:
                            row_std((hf, 1, SIDE[hf][u + 2]))
                        if last and u == UNITS - 4:
                            row_std((hf, 2, 0))
                        if last and u == UNITS:
                            row_high((hf, 2, 0))
                            row_std((hf, 2, 1))
                        h = (u - WO_SPLIT) % UNITS
                        if h < REP and (not last or u < UNITS):
                            split_hi(raw[:, h % 2, :], raw_in[h % 2],
                                     p0 + (u - WO_SPLIT) // UNITS * REP + h // 2 + 1, wo_s[:, h, HI, :])
                        h = u - WQ_SPLIT
                        if h in range(REP) and not last:
                            split_hi(raw[:, h % 2, :], raw_in[h % 2], p0 + REP // 2 + h // 2 + 1,
                                     wq_s[:, h, :, HI, :])

                step(0, range(1), first=True)
                if hf == 0:
                    row_high((0, 1, 3))
                step(0, range(1, 2), first=True)
                if hf == 0:
                    row_high((0, 1, 4))
                step(0, range(2, UNITS + LAG), first=True)
                with act.Fori(1, HKV - 1) as g:
                    step(g, range(LAG, UNITS + LAG))
                step(HKV - 1, range(LAG, UNITS + LAG), last=True)

                for t in range(HT):
                    if hf + 1 < NH and t >= LN_LAG:
                        row_std((hf + 1, 1, t - LN_LAG))
                    if t + 1 < HT:
                        row_high((hf, 2, t + 1))
                    if t + 2 < HT:
                        row_std((hf, 2, t + 2))
                    if hf + 1 < NH:
                        if t == HT - 1:
                            for h in range(REP):
                                act.wait_ge(w4_used, hf * REP + h + 1)
                                if h < 2:
                                    first_weights(seen + HALF_PIECES // 2, h)
                        if t >= LN_LAG:
                            row_high((hf + 1, 1, t - LN_LAG))

            for hf in range(NH):
                half(hf)

        @block.vector
        def _(dve):
            dve.sem_inc(rope_sind, 2)
            dve.sem_inc(rope_lo, 2)
            dve.sem_inc(wide_free, BURST)
            dve.sem_inc(s_read, 1)
            dve.sem_inc(pT_lo, 1)
            dve.sem_inc(o_lo, 1)
            dve.sem_inc(stage_lo, STAGED // 2)
            H2 = DK // 2

            def rope_turn(n, slot=0):
                src, _, dst = ropes[slot]
                dve.wait_ge(rope_in, 2 + n + 1)
                dve.tensor_tensor(dst[0:H2], src[H2:DK], sin_t[H2:DK, :], ALU.mult)
                dve.tensor_tensor(dst[H2:DK], src[0:H2], sin_t[0:H2, :], ALU.mult).then_inc(rope_sind, 1)

            def rope_add(n, slot=0):
                _, total, second = ropes[slot]
                dve.wait_ge(rope_cosd, 2 + n + 1)
                dve.wait_ge(rope_sind, 2 + n + 1)
                dve.tensor_tensor(total, total, second, ALU.add).then_inc(rope_sum, 1)

            def rope_low(n, parts, slot=0):
                dve.wait_ge(rope_hi, n + 1)
                dve.tensor_tensor(parts[:, LO, :], ropes[slot][1], parts[:, HI, :].bitcast(F32),
                                  ALU.subtract).then_inc(rope_lo, 1)

            def context_low(first, j):
                dve.wait_ge(ctx_hi, first + j + 1)
                dve.tensor_tensor(ctxT[:, 2 * j:2 * j + 2, LO, :],
                                  ctx_ps[j][:, :].rearrange("p (c n) -> p c n", c=2),
                                  ctxT[:, 2 * j:2 * j + 2, HI, :].bitcast(F32),
                                  ALU.subtract).then_inc(ctx_lo, 1)

            def decode_codes(steps, loaded):
                dve.wait_ge(planes_in, loaded)
                for r in range(4):
                    last = dve.tensor_scalar(spread[:, r], planes, r, 0x11111111,
                                             ALU.logical_shift_right, ALU.bitwise_and)
                steps.mark(last)
                for k in range(1, BITS):
                    steps.wait()
                    steps.mark(dve.scalar_tensor_tensor(
                        nibbles, spread[:, :, k, :], k, spread[:, :, 0, :] if k == 1 else nibbles,
                        ALU.logical_shift_left, ALU.bitwise_or))
                steps.wait()
                place = codes.rearrange("p (w j r) -> p j r w", j=8, r=4)
                for j in range(8):
                    last = dve.tensor_scalar(place[:, j], nibbles, 4 * j, LEVELS - 1,
                                             ALU.logical_shift_right, ALU.bitwise_and)
                steps.mark(last)

            ln_steps = Steps(dve, ln_step, 0)

            def row_stats(key):
                hf, layer, t = key
                s = LN[key] % 2
                if layer == 1:
                    dve.wait_ge(x_in[t], 16 * (hf + 1))
                for n in range(NN):
                    last = dve.bn_stats(ln_stat[:, s, n, :], acc[:, t, n * BANK:(n + 1) * BANK])
                ln_steps.mark(last)
                ln_steps.wait()
                ln_steps.mark(dve.bn_aggr(ln_mv[:, s, :], ln_stat[:, s, :, :].rearrange("p n k -> p (n k)")))
                ln_steps.wait()
                dve.tensor_scalar(ln_ve[:, s:s + 1], ln_mv[:, s, 1:2], EPS, None, ALU.add).then_inc(ln_var, 1)

            def rows(key):
                s = LN[key] % 2
                col = slice(s, s + 1)
                dve.wait_ge(ln_std, LN[key] + 1)
                ln_steps.mark(dve.reciprocal(ln_y[:, col], ln_sd[:, col]))
                ln_steps.wait()
                ln_steps.mark(dve.tensor_scalar(ln_e[:, col], ln_y[:, col], ln_y[:, col], ln_ve[:, col],
                                                ALU.mult, ALU.mult))
                ln_steps.wait()
                ln_steps.mark(dve.tensor_scalar(ln_f[:, col], ln_e[:, col], -0.5, 1.5, ALU.mult, ALU.add))
                ln_steps.wait()
                ln_steps.mark(dve.tensor_tensor(ln_r[:, col], ln_y[:, col], ln_f[:, col], ALU.mult))
                ln_steps.wait()
                if LN[key]:
                    dve.wait_ge(ln_tr, LN[key])
                dve.tensor_scalar(ln_row[:, :], acc[:, key[2], :], ln_mv[:, s, 0:1], ln_r[:, col],
                                  ALU.subtract, ALU.mult).then_inc(ln_rows, 1)

            def rows_low(key, chunks, src):
                t = key[2]
                part = xT[:, chunks:chunks + 4, :, t * P:(t + 1) * P]
                return dve.tensor_tensor(part[:, :, LO, :], src[:, :].rearrange("p (c n) -> p c n", c=4),
                                         part[:, :, HI, :].bitcast(F32), ALU.subtract)

            def row_low(key):
                dve.wait_ge(ln_hi, LN_SPLIT[key])
                for j in range(2):
                    last = rows_low(key, 4 * j, ln_ps[key][j])
                last.then_inc(ln_lo, 1)

            for j in range(4):
                context_low(0, j)
            for k in range(A_PIECES):
                if C <= k < C + POOL_PIECES:
                    continue
                parts = (wk_s, wv_s)[k // C][:, k % C]
                dve.wait_ge(w_hi, k + 1)
                dve.tensor_tensor(parts[:, LO, :], a_raw[k % A_SLOTS], parts[:, HI, :].bitcast(F32),
                                  ALU.subtract).then_inc(w_lo, 1)
            dve.wait_ge(wv_lo, POOL_PIECES)
            decode_codes(Steps(dve, dq_step, 0), 16)
            dve.wait_ge(tables_in, 32)

            def batch(b, last=False):
                steps = Steps(dve, dq_step, CODE_STEPS + b * DQ_STEPS)

                def level_term(dst, level):
                    return dve.tensor_scalar(dst, codes, float(level), lut_t[:, level:level + 1],
                                             ALU.is_equal, ALU.mult)

                def pool_term(i):
                    if i >= 3:
                        dve.wait_ge(term_used, b * POOL_LEVELS + i - 1)
                    level_term(term_p[i % 2] if i else sum_p, i).then_inc(term_ready, 1)

                def vector_term(i):
                    if i == 0:
                        steps.mark(level_term(sum_v, POOL_LEVELS))
                    else:
                        steps.wait()
                        steps.mark(level_term(term_v, POOL_LEVELS + i))
                        steps.wait()
                        steps.mark(dve.tensor_tensor(sum_v, sum_v, term_v, ALU.add))

                def staged_low(i, src):
                    stage = staging(i)[0]
                    dve.wait_ge(stage_hi, b * STAGED + i + 1)
                    dve.tensor_tensor(stage[:, BANK:2 * BANK], src[:, :], stage[:, 0:BANK].bitcast(F32),
                                      ALU.subtract).then_inc(stage_lo, 1)

                dve.wait_ge(lut_in, 16 * (b + 1))
                steps.wait()
                beside = ((0, 1), (2,), (3,), (), (4,), (5,), (), (6,))
                for g in range(HKV):
                    rope_turn(b * HKV + g, g % 2)
                    if g:
                        rope_low(b * HKV + g - 1, k_stage[:, (g - 1) % 2], (g - 1) % 2)
                    rope_add(b * HKV + g, g % 2)
                    for i in beside[g]:
                        pool_term(i)
                    if g in (3, 6):
                        vector_term(g // 3 - 1)
                rope_low(b * HKV + HKV - 1, k_stage[:, (HKV - 1) % 2], (HKV - 1) % 2)
                vector_term(2)
                pool_term(7)
                pool_term(8)
                staged_low(V0, wide_ps[0])
                vector_term(3)
                pool_term(9)
                vector_term(4)
                pool_term(10)
                staged_low(V1, wide_ps[1])
                if last:
                    row_stats((0, 1, 0))
                    row_stats((0, 1, 1))
                steps.wait()
                dve.wait_ge(term_used, (b + 1) * POOL_LEVELS)
                dve.tensor_tensor(sum_v, sum_v, sum_p, ALU.add).then_inc(w4_ready, 1)
                if last:
                    rows((0, 1, 0))
                staged_low(V2, wide_ps[0])
                staged_low(D0, w4_ps[0])
                if not last:
                    context_low(4 * (b + 1), 0)
                else:
                    rows((0, 1, 1))
                    row_low((0, 1, 0))
                    row_low((0, 1, 1))
                staged_low(D1, w4_ps[1])
                if not last:
                    for j in range(1, 4):
                        context_low(4 * (b + 1), j)
                staged_low(V3, wide_ps[1])
                if last:
                    row_stats((0, 1, 2))
                    row_stats((0, 1, 3))
                    rows((0, 1, 2))
                if not last:
                    decode_codes(steps, 16 * (b + 2))
                    assert steps.n == DQ_STEPS

            with dve.Fori(0, NB - 1) as b:
                batch(b)
            batch(NB - 1, last=True)

            def half(hf):
                wide0 = A_WIDE + hf * HALF_WIDE
                r_half = A_ROPES + hf * HALF_UNITS
                rope_turn(r_half)
                rope_add(r_half)
                rope_low(r_half, q_s[:, 0])
                if hf == 0:
                    row_stats((0, 1, 4))
                rope_turn(r_half + 1)
                rope_add(r_half + 1)
                if hf == 0:
                    rows((0, 1, 3))
                rope_low(r_half + 1, q_s[:, 1])

                def step(g, units, first=False, last=False):
                    n0 = hf * HALF_UNITS + g * UNITS
                    w0 = wide0 + g * HB * BURST
                    r0 = r_half + g * UNITS

                    def add_mask(u):
                        if u % REP == 0:
                            dve.wait_ge(mask_in, 16 * (hf * HKV * HB + g * HB + u // REP + 1))
                        dve.wait_ge(pT_tr, n0 + u + 1)
                        dve.wait_ge(s_mm, 1 + n0 + u + 1)
                        hold(dve)
                        for t in range(TS):
                            last = dve.tensor_tensor_reduce(
                                out=probs[:, u % 2, t, :], in0=s_ps[:, t * S:(t + 1) * S],
                                in1=mask_t[:, t, :], scale=1.0, scalar=-3.0e38, op0=ALU.add, op1=ALU.max,
                                accum_out=row_max[:, u % 2, t:t + 1])
                        last.then_inc(s_read, 1)
                        dve.wait_ge(s_read, 1 + n0 + u + 1)
                        dve.tensor_scalar(neg_max[:, u % 2, :], row_max[:, u % 2, :], -1.0, None,
                                          ALU.mult).then_inc(s_max, 1)

                    def invert(u):
                        dve.wait_ge(exp_done, n0 + u + 1)
                        dve.reciprocal(row_inv[:, u % 2, :], row_sum[:, u % 2, :]).then_inc(inv_ready, 1)

                    def turned_low(u):
                        dve.wait_ge(pT_hi, n0 + u + 1)
                        dve.tensor_tensor(pT_s[:, LO, :, :], pT_ps[:, :].rearrange("p (k n) -> p k n", k=TS),
                                          pT_s[:, HI, :, :].bitcast(F32), ALU.subtract).then_inc(pT_lo, 1)

                    def output_low(u):
                        dve.wait_ge(o_hi, n0 + u + 1)
                        dve.tensor_tensor(o_s[:, u % 2, LO, :], o_ps, o_s[:, u % 2, HI, :].bitcast(F32),
                                          ALU.subtract).then_inc(o_lo, 1)

                    def add_projection(b):
                        for t in range(TS):
                            for n in range(NN):
                                dve.wait_ge(wide_mm, w0 + b * BURST + t * NN + n + 1)
                                part = acc[:, b * TS + t, n * BANK:(n + 1) * BANK]
                                dve.tensor_tensor(part, part, out_ps[t * NN + n][:, :],
                                                  ALU.add).then_inc(wide_free, 1)

                    def side_low(key, j):
                        dve.wait_ge(side_hi, 2 * LN_SIDE.index(key) + j + 1)
                        rows_low(key, 4 * j, pT_ps).then_inc(side_lo, 1)

                    for u in units:
                        short = last and u + AHEAD >= UNITS
                        if short and u - 2 < UNITS:
                            output_low(u - 2)
                        if not last or u < UNITS:
                            add_mask(u)
                        if first and hf == 0 and u + 2 in (2, 3, 4):
                            row_low((0, 1, u + 2))
                        if first and hf == 0 and u == 0:
                            rows((0, 1, 4))
                        if first and beside(hf, u):
                            side_low(*beside(hf, u))
                        if first and u + 1 in SIDE[hf]:
                            rows((hf, 1, SIDE[hf][u + 1]))
                        if short and u - 1 < UNITS:
                            turned_low(u - 1)
                        if not last or u < UNITS:
                            invert(u)
                        if not short:
                            rope_turn(r0 + u + AHEAD)
                            if u >= 2:
                                output_low(u - 2)
                            if u >= 1:
                                turned_low(u - 1)
                            rope_add(r0 + u + AHEAD)
                            rope_low(r0 + u + AHEAD, q_s[:, (u + AHEAD) % 4])
                        if u >= LAG and (u - LAG) % REP == REP - 1:
                            add_projection((u - LAG) // REP)
                        if first and u + 2 in SIDE[hf]:
                            row_stats((hf, 1, SIDE[hf][u + 2]))
                        if last and u == UNITS - 4:
                            row_stats((hf, 2, 0))
                        if last and u == UNITS - 3:
                            rows((hf, 2, 0))
                        if last and u == UNITS:
                            row_low((hf, 2, 0))
                            row_stats((hf, 2, 1))
                        if last and u == UNITS + 1:
                            rows((hf, 2, 1))

                step(0, range(UNITS + LAG), first=True)
                with dve.Fori(1, HKV - 1) as g:
                    step(g, range(LAG, UNITS + LAG))
                step(HKV - 1, range(LAG, UNITS + LAG), last=True)

                wide_c = wide0 + HKV * HB * BURST

                def add_layer(t):
                    dve.wait_ge(biased, hf * HT + t + 1)
                    for n in range(NN):
                        dve.wait_ge(wide_mm, wide_c + t * NN + n + 1)
                        part = acc[:, t, n * BANK:(n + 1) * BANK]
                        dve.tensor_tensor(part, part, out_ps[t % 2 * NN + n][:, :], ALU.add).then_inc(wide_free, 1)
                    dve.wait_ge(wide_free, BURST + wide_c - A_WIDE + (t + 1) * NN)
                    dve.sem_inc(out_ready, 1)

                for t in range(HT):
                    o = t - LN_LAG
                    if t >= 1:
                        add_layer(t - 1)
                    if hf + 1 < NH and o >= 1:
                        row_low((hf + 1, 1, o - 1))
                    if hf + 1 < NH and o >= 0:
                        row_stats((hf + 1, 1, o))
                        rows((hf + 1, 1, o))
                    if t + 1 < HT:
                        row_low((hf, 2, t + 1))
                    if t + 2 < HT:
                        row_stats((hf, 2, t + 2))
                        rows((hf, 2, t + 2))
                add_layer(HT - 1)
                if hf + 1 < NH:
                    row_low((hf + 1, 1, HT - LN_LAG - 1))

            for hf in range(NH):
                half(hf)

        @block.gpsimd
        def _(pool):
            pool.sem_inc(rope_cosd, 2)
            for s in range(2):
                pool.sem_inc(k_stored[s], 16)
            pool.sem_inc(v_stored, 16)
            pool.memset(ident[:, :], 0.0).then_inc(ident_step, 1)
            pool.wait_ge(ident_step, 1)
            pool.affine_select(out=ident[:, :], in_=ident[:, :], compare_op=ALU.not_equal, fill=1.0, base=0,
                               pattern=[[-1, P]], channel_multiplier=1).then_inc(ident_ok, 1)

            def rope_first(n, slot=0, slots=1):
                pool.wait_ge(rope_lo, 2 + n - slots + 1)
                pool.wait_ge(rope_in, 2 + n + 1)
                pool.tensor_tensor(ropes[slot][1], ropes[slot][0], cos_t[:, :], ALU.mult).then_inc(rope_cosd, 1)

            def split_lo(k, slot, parts_hi, parts_lo):
                pool.wait_ge(w_hi, k + 1)
                src = raw[:, slot, :]
                if len(parts_hi.shape) == 3:
                    src = src.rearrange("p (c n) -> p c n", c=C)
                pool.tensor_tensor(parts_lo, src, parts_hi.bitcast(F32), ALU.subtract).then_inc(w_lo, 1)

            for k in range(C, C + POOL_PIECES):
                parts = wv_s[:, k % C]
                pool.wait_ge(w_hi, k + 1)
                pool.tensor_tensor(parts[:, LO, :], a_raw[k % A_SLOTS], parts[:, HI, :].bitcast(F32),
                                   ALU.subtract).then_inc(wv_lo, 1)
            pool.wait_ge(tables_in, 32)

            def batch(b):
                def add_term(i):
                    pool.wait_ge(term_ready, b * POOL_LEVELS + i + 1)
                    if i == 0:
                        pool.sem_inc(term_used, 1)
                    else:
                        pool.wait_ge(term_used, b * POOL_LEVELS + i)
                        pool.tensor_tensor(sum_p, sum_p, term_p[i % 2], ALU.add).then_inc(term_used, 1)

                beside = ((0,), (1,), (2,), (), (3,), (4,), (), (5,))
                for g in range(HKV):
                    rope_first(b * HKV + g, g % 2, 2)
                    for i in beside[g]:
                        add_term(i)
                for i in range(6, POOL_LEVELS):
                    add_term(i)

            with pool.Fori(0, NB - 1) as b:
                batch(b)
            batch(NB - 1)

            def first_weights(hf, h):
                split_lo(A_PIECES + hf * HALF_PIECES + h, h % 2, wq_s[:, h, :, HI, :], wq_s[:, h, :, LO, :])

            for h in range(2):
                first_weights(0, h)

            def half(hf):
                piece = A_PIECES + hf * HALF_PIECES
                r_half = A_ROPES + hf * HALF_UNITS
                rope_first(r_half)
                first_weights(hf, 2)
                rope_first(r_half + 1)
                first_weights(hf, 3)

                def step(g, units, last=False):
                    n0 = hf * HALF_UNITS + g * UNITS
                    r0 = r_half + g * UNITS
                    p0 = piece + REP + g * 2 * REP
                    for u in units:
                        if not last or u < UNITS:
                            pool.wait_ge(inv_ready, n0 + u + 1)
                            hold(pool)
                            for t in range(TS):
                                done = pool.tensor_scalar(probs[:, u % 2, t, :], probs[:, u % 2, t, :],
                                                          row_inv[:, u % 2, t:t + 1], 1.0, ALU.mult, ALU.mult)
                            done.then_inc(p_ready, 1)
                        if not last or u + AHEAD < UNITS:
                            rope_first(r0 + u + AHEAD)
                        h = (u - WO_SPLIT) % UNITS
                        if h < REP and (not last or u < UNITS):
                            split_lo(p0 + (u - WO_SPLIT) // UNITS * 2 * REP + h, h % 2,
                                     wo_s[:, h, HI, :], wo_s[:, h, LO, :])
                        h = u - WQ_SPLIT
                        if h in range(REP) and not last:
                            split_lo(p0 + REP + h, h % 2, wq_s[:, h, :, HI, :], wq_s[:, h, :, LO, :])

                step(0, range(UNITS + LAG))
                with pool.Fori(1, HKV - 1) as g:
                    step(g, range(LAG, UNITS + LAG))
                step(HKV - 1, range(LAG, UNITS + LAG), last=True)

                pool.wait_ge(bias_in, 16 * (hf + 1))
                for t in range(HT):
                    pool.wait_ge(ln_rows, LN[hf, 2, t] + 1)
                    pool.tensor_tensor(acc[:, t, :], acc[:, t, :], bias_t, ALU.add).then_inc(biased, 1)
                if hf + 1 < NH:
                    for h in range(2):
                        first_weights(hf + 1, h)

            for hf in range(NH):
                half(hf)


_INS = ("x", "ctx_4096", "mask_BxSxS2_ff0", "L0_xattn_wq", "L0_xattn_wk", "L0_xattn_wv", "L0_xattn_wo",
        "L0_ffn_qweight", "L0_ffn_lut4", "L0_ffn_bias")


def _rope_tables(positions, width):
    import numpy as np

    f = np.float32
    inv = f(1.0) / np.power(f(10000.0), np.arange(0, width, 2, dtype=f) / f(width))
    angle = (np.arange(positions, dtype=f)[None, :] * inv.astype(f)[:, None]).astype(f)
    cos, sin = np.cos(angle).astype(f), np.sin(angle).astype(f)
    return np.concatenate([cos, cos]), np.concatenate([sin, -sin])


def kernel(**inputs):
    import numpy as np
    import concourse.bacc as bacc
    from concourse import mybir
    from concourse.bass_utils import run_bass_kernel_spmd

    nc = bacc.Bacc("TRN2", target_bir_lowering=False, num_devices=1)
    arrays = {name: np.ascontiguousarray(inputs[name]) for name in _INS}
    shape = arrays["x"].shape
    arrays["rope_cos"], arrays["rope_sin"] = _rope_tables(shape[1], 128)
    args = [nc.dram_tensor(f"in_{n}", a.shape, mybir.dt.from_np(a.dtype), kind="ExternalInput").ap()
            for n, a in arrays.items()]
    out = nc.dram_tensor("out_y", shape, mybir.dt.float32, kind="ExternalOutput").ap()
    build_xattn_ffn(nc, *args, out)
    r = run_bass_kernel_spmd(nc, [{f"in_{n}": a for n, a in arrays.items()}], core_ids=[0])
    return r.results[0]["out_y"]
```
